# Optimizing a Trainium2 kernel written in Bass

```python
import numpy as np
import jax
import jax.numpy as jnp

def _softmax(x, axis=-1):
    return jax.nn.softmax(x, axis=axis)

def _gelu(x):
    return jax.nn.gelu(x, approximate=True)

def _silu(x):
    return jax.nn.silu(x)

def _sigmoid(x):
    return jax.nn.sigmoid(x)

def _layernorm(x, axis=-1, eps=1e-05):
    m = jnp.mean(x, axis=axis, keepdims=True)
    v = jnp.var(x, axis=axis, keepdims=True)
    return (x - m) / jnp.sqrt(v + eps)

def _scatter_add(tgt, idx, src, axis=0):
    return tgt.at[idx].add(src)

def _segment_sum(src, seg, n):
    return jax.ops.segment_sum(src, seg, n)
kernel_name = 'mk_gnn_preln_d2_gnn_r32_ec9886'

def setup_inputs(seed: int=0):
    np.random.seed(seed)
    _w = jnp.asarray

    def _rec_inputs():
        import jax
        import jax.numpy as jnp
        _gk = jax.random.key(seed)
        x = -0.0003713 + 1 * jax.random.normal(jax.random.fold_in(_gk, 1), (3125, 128), jnp.float32)
        _s = jax.random.randint(jax.random.fold_in(_gk, 2), (25000,), 0, 3125, jnp.int32)
        _d = jax.random.randint(jax.random.fold_in(_gk, 3), (25000,), 0, 3125, jnp.int32)
        _loop = jnp.arange(3125, dtype=jnp.int32)
        src = jnp.concatenate([_s, _d, _loop])
        dst = jnp.concatenate([_d, _s, _loop])
        _o = jnp.argsort(dst, stable=True)
        src = src[_o]
        dst = dst[_o]
        edge_type_8 = jax.random.randint(jax.random.fold_in(_gk, 13), (53125,), 0, 8, jnp.int32)
        edge_weight = jax.random.uniform(jax.random.fold_in(_gk, 14), (53125,), jnp.float32, 0.0, 0.999998)
        return (x, src, dst, edge_type_8, edge_weight)
    x, src, dst, edge_type_8, edge_weight = _rec_inputs()

    def _L0_gnn_setup():
        import jax, jax.numpy as jnp
        import numpy as np
        N = 3125
        E = 50000
        D_IN = 128
        H = 2
        C = 64

        def segment_softmax(e, dst, n):
            m = jax.ops.segment_max(e, dst, num_segments=n)
            m = jnp.where(jnp.isfinite(m), m, 0.0)
            p = jnp.exp(e - m[dst])
            s = jax.ops.segment_sum(p, dst, num_segments=n)
            return p / (s[dst] + 1e-16)

        def gat_conv(x, W, a_src, a_dst, b, src, dst, n):
            h = (x @ W).reshape(n, H, C)
            asrc = jnp.einsum('nhc,hc->nh', h, a_src)
            adst = jnp.einsum('nhc,hc->nh', h, a_dst)
            e = jax.nn.leaky_relu(asrc[src] + adst[dst], 0.2)
            alpha = segment_softmax(e, dst, n)
            msg = h[src] * alpha[:, :, None]
            out = jax.ops.segment_sum(msg, dst, num_segments=n)
            return out.reshape(n, H * C) + b
        key = jax.random.key(seed)
        k = jax.random.split(key, 9)
        s1 = 1.0 / np.sqrt(D_IN)
        s2 = 1.0 / np.sqrt(H * C)
        return {'x': jax.random.normal(k[0], (N, D_IN), jnp.float32), 'edge_index': jax.random.randint(k[1], (2, E), 0, N, jnp.int32), 'W1': jax.random.normal(k[2], (D_IN, H * C), jnp.float32) * s1, 'a_src1': jax.random.normal(k[3], (H, C), jnp.float32) * s2, 'a_dst1': jax.random.normal(k[4], (H, C), jnp.float32) * s2, 'b1': jnp.zeros((H * C,), jnp.float32), 'W2': jax.random.normal(k[5], (H * C, H * C), jnp.float32) * s2, 'a_src2': jax.random.normal(k[6], (H, C), jnp.float32) * s2, 'a_dst2': jax.random.normal(k[7], (H, C), jnp.float32) * s2, 'b2': jnp.zeros((H * C,), jnp.float32)}
    _L0_gnn_all = _L0_gnn_setup()
    _L0_gnn_in = {k: v for k, v in _L0_gnn_all.items() if k in ('W1', 'a_src1', 'a_dst1', 'b1', 'W2', 'a_src2', 'a_dst2', 'b2')}
    del _L0_gnn_all

    def _L1_gnn_setup():
        import jax, jax.numpy as jnp
        import numpy as np
        N_NODES = 50000
        N_EDGES = 25000
        IN_DIM = 128
        H_DIM = 128
        NUM_RELS = 8

        def _rel_graph_conv(x, src, dst, etypes, norm, comp, V, bias):
            W = jnp.einsum('rb,bio->rio', comp, V)
            H = jnp.einsum('ni,rio->nro', x, W)
            m = H[src, etypes] * norm
            agg = jax.ops.segment_sum(m, dst, num_segments=x.shape[0])
            return agg + bias
        key = jax.random.key(seed)
        ks = jax.random.split(key, 10)
        s_in = 1.0 / np.sqrt(IN_DIM)
        s_h = 1.0 / np.sqrt(H_DIM)
        return {'features': jax.random.normal(ks[0], (N_NODES, IN_DIM), jnp.float32), 'etypes': jax.random.randint(ks[1], (N_EDGES,), 0, NUM_RELS), 'edge_weight': jax.random.uniform(ks[2], (N_EDGES,), jnp.float32), 'src': jax.random.randint(ks[3], (N_EDGES,), 0, N_NODES), 'dst': jax.random.randint(ks[4], (N_EDGES,), 0, N_NODES), 'comp1': jax.random.normal(ks[5], (NUM_RELS, NUM_RELS), jnp.float32) * (1.0 / NUM_RELS), 'V1': jax.random.normal(ks[6], (NUM_RELS, IN_DIM, H_DIM), jnp.float32) * s_in, 'bias1': jnp.zeros((H_DIM,), jnp.float32), 'comp2': jax.random.normal(ks[7], (NUM_RELS, NUM_RELS), jnp.float32) * (1.0 / NUM_RELS), 'V2': jax.random.normal(ks[8], (NUM_RELS, H_DIM, H_DIM), jnp.float32) * s_h, 'bias2': jnp.zeros((H_DIM,), jnp.float32)}
    _L1_gnn_all = _L1_gnn_setup()
    _L1_gnn_in = {k: v for k, v in _L1_gnn_all.items() if k in ('comp1', 'V1', 'bias1', 'comp2', 'V2', 'bias2')}
    del _L1_gnn_all
    return {'x': x, 'src': src, 'dst': dst, 'edge_type_8': edge_type_8, 'edge_weight': edge_weight, 'L0_gnn_W1': _L0_gnn_in['W1'], 'L0_gnn_a_src1': _L0_gnn_in['a_src1'], 'L0_gnn_a_dst1': _L0_gnn_in['a_dst1'], 'L0_gnn_b1': _L0_gnn_in['b1'], 'L0_gnn_W2': _L0_gnn_in['W2'], 'L0_gnn_a_src2': _L0_gnn_in['a_src2'], 'L0_gnn_a_dst2': _L0_gnn_in['a_dst2'], 'L0_gnn_b2': _L0_gnn_in['b2'], 'L1_gnn_comp1': _L1_gnn_in['comp1'], 'L1_gnn_V1': _L1_gnn_in['V1'], 'L1_gnn_bias1': _L1_gnn_in['bias1'], 'L1_gnn_comp2': _L1_gnn_in['comp2'], 'L1_gnn_V2': _L1_gnn_in['V2'], 'L1_gnn_bias2': _L1_gnn_in['bias2']}

def reference(x, src, dst, edge_type_8, edge_weight, L0_gnn_W1, L0_gnn_a_src1, L0_gnn_a_dst1, L0_gnn_b1, L0_gnn_W2, L0_gnn_a_src2, L0_gnn_a_dst2, L0_gnn_b2, L1_gnn_comp1, L1_gnn_V1, L1_gnn_bias1, L1_gnn_comp2, L1_gnn_V2, L1_gnn_bias2):
    import jax
    import jax.numpy as jnp

    def _L0_gnn_ref(x, edge_index, W1, a_src1, a_dst1, b1, W2, a_src2, a_dst2, b2):
        import jax, jax.numpy as jnp
        import numpy as np
        N = 3125
        E = 50000
        D_IN = 128
        H = 2
        C = 64

        def segment_softmax(e, dst, n):
            m = jax.ops.segment_max(e, dst, num_segments=n)
            m = jnp.where(jnp.isfinite(m), m, 0.0)
            p = jnp.exp(e - m[dst])
            s = jax.ops.segment_sum(p, dst, num_segments=n)
            return p / (s[dst] + 1e-16)

        def gat_conv(x, W, a_src, a_dst, b, src, dst, n):
            h = (x @ W).reshape(n, H, C)
            asrc = jnp.einsum('nhc,hc->nh', h, a_src)
            adst = jnp.einsum('nhc,hc->nh', h, a_dst)
            e = jax.nn.leaky_relu(asrc[src] + adst[dst], 0.2)
            alpha = segment_softmax(e, dst, n)
            msg = h[src] * alpha[:, :, None]
            out = jax.ops.segment_sum(msg, dst, num_segments=n)
            return out.reshape(n, H * C) + b
        loops = jnp.arange(N, dtype=edge_index.dtype)
        ei = jnp.concatenate([edge_index, jnp.stack([loops, loops])], axis=1)
        src, dst = (ei[0], ei[1])
        h = jax.nn.relu(gat_conv(x, W1, a_src1, a_dst1, b1, src, dst, N))
        out = jax.nn.relu(gat_conv(h, W2, a_src2, a_dst2, b2, src, dst, N))
        return out

    def _L1_gnn_ref(features, etypes, edge_weight, src, dst, comp1, V1, bias1, comp2, V2, bias2):
        import jax, jax.numpy as jnp
        import numpy as np
        N_NODES = 50000
        N_EDGES = 25000
        IN_DIM = 128
        H_DIM = 128
        NUM_RELS = 8

        def _rel_graph_conv(x, src, dst, etypes, norm, comp, V, bias):
            W = jnp.einsum('rb,bio->rio', comp, V)
            H = jnp.einsum('ni,rio->nro', x, W)
            m = H[src, etypes] * norm
            agg = jax.ops.segment_sum(m, dst, num_segments=x.shape[0])
            return agg + bias
        norm = edge_weight[:, None]
        h = _rel_graph_conv(features, src, dst, etypes, norm, comp1, V1, bias1)
        h = jax.nn.relu(h)
        h = _rel_graph_conv(h, src, dst, etypes, norm, comp2, V2, bias2)
        return h
    edge_index = jnp.stack([src, dst])
    h = jnp.maximum(_layernorm(x, axis=-1), 0.0)
    x = x + _L0_gnn_ref(h, edge_index, L0_gnn_W1, L0_gnn_a_src1, L0_gnn_a_dst1, L0_gnn_b1, L0_gnn_W2, L0_gnn_a_src2, L0_gnn_a_dst2, L0_gnn_b2)
    h = jnp.maximum(_layernorm(x, axis=-1), 0.0)
    x = x + _L1_gnn_ref(h, edge_type_8, edge_weight, src, dst, L1_gnn_comp1, L1_gnn_V1, L1_gnn_bias1, L1_gnn_comp2, L1_gnn_V2, L1_gnn_bias2)
    return x

_drawn_inputs = setup_inputs


def setup_inputs(seed=0):
    import zlib

    import numpy as np

    out = dict(_drawn_inputs(seed))
    spreads = {'L0_gnn_b1': (0.0, 0.1),
     'L0_gnn_b2': (0.0, 0.1),
     'L1_gnn_bias1': (0.0, 0.1),
     'L1_gnn_bias2': (0.0, 0.1)}
    factors = {'L0_gnn_a_src1': 3.448, 'L0_gnn_a_dst1': 8.0, 'L0_gnn_a_src2': 8.0, 'L0_gnn_a_dst2': 8.0}
    for name, (base, spread) in spreads.items():
        noise = np.random.default_rng([zlib.crc32(name.encode()), seed]).standard_normal(out[name].shape)
        drawn = base * np.exp(spread * noise) if base else spread * noise
        out[name] = jnp.asarray(drawn.astype(out[name].dtype))
    for name, factor in factors.items():
        out[name] = (out[name] * factor).astype(out[name].dtype)
    return out
```

```python
from contextlib import ExitStack

import concourse.bass as bass
from concourse import mybir

F32 = mybir.dt.float32
I32 = mybir.dt.int32
ALU = mybir.AluOpType
ACT = mybir.ActivationFunctionType
AX = mybir.AxisListType.X

N = 3125
E = 53125
D = 128
H = 2
C = D // H
R = 8
TN = 121
NT = -(-N // TN)
PAIRS = NT // 2
LAST = N - (NT - 1) * TN
T = 17
CH = 128 * T
MAXC = -(-E // CH)
EC = -(-E // 128)
EFULL = E // EC
EREST = E - EFULL * EC
PADC = 425
EPAD = 128 * (EC + PADC)
GW = 132
HW = 134
GRP = 4
NG = -(-T // GRP)
EPS_LN = 1e-5
SLOPE = 0.2
FAR = 1e30

assert NT == 2 * PAIRS and EPAD >= E + MAXC * CH and 0 < EREST < EC


def groups():
    return [(k, k * GRP, min(T, (k + 1) * GRP)) for k in range(NG)]


def build(nc, x, src, dst, etype, eweight, W1, as1, ad1, b1, W2, as2, ad2, b2,
          comp1, V1, c1, comp2, V2, c2, out):
    with ExitStack() as ctx:
        def sb(name, shape, dt=F32):
            return ctx.enter_context(nc.sbuf_tensor(name, shape, dt))

        def ps(name):
            return ctx.enter_context(nc.psum_tensor(name, [128, 512], F32))

        def sem(name):
            return ctx.enter_context(nc.semaphore(name))

        records = nc.dram_tensor("records", (EPAD, 4), I32).ap()
        gat_rows = [nc.dram_tensor(f"gat_rows{l}", (NT * TN, GW), F32).ap() for l in range(2)]
        rel_rows = [nc.dram_tensor(f"rel_rows{l}", (NT * TN * R, D), F32).ap() for l in range(2)]

        ident = sb("ident", [128, 128])
        ones = sb("ones", [128, 128])
        pick = sb("pick", [T, T, TN])
        iota_i = sb("iota_i", [128, TN], I32)
        iota = sb("iota", [128, TN])
        base_i = sb("base_i", [128, NT + 1], I32)
        base = sb("base", [128, NT + 1])
        w1 = sb("w1", [128, D + 4])
        w2 = sb("w2", [128, D + 4])
        score1 = sb("score1", [128, 4, C])
        score2 = sb("score2", [128, 4, C])
        prod = sb("prod", [128, D])
        bias = sb("bias", [128, 4, D])
        comp = sb("comp", [128, 2, R * R])
        V = sb("V", [128, R, D])
        rel_w = [sb(f"rel_w{l}", [128, R, D]) for l in range(2)]

        src_all = sb("src_all", [128, EC], I32)
        dst_all = sb("dst_all", [128, EC], I32)
        nxt_all = sb("nxt_all", [128, EC], I32)
        typ_all = sb("typ_all", [128, EC], I32)
        wgt_all = sb("wgt_all", [128, EC])
        dst_f = sb("dst_f", [128, EC])
        nxt_f = sb("nxt_f", [128, EC])
        scratch = sb("scratch", [128, EC])
        rec_all = sb("rec_all", [128, EC, 4], I32)
        rec_pad = sb("rec_pad", [128, PADC, 4], I32)
        counts = sb("counts", [128, NT + 2])
        row = sb("row", [1, 8, NT + 2])
        steps_i = sb("steps_i", [1, MAXC - 1], I32)
        steps = sb("steps", [1, MAXC - 1])
        over = sb("over", [1, PAIRS, MAXC - 1])
        plan = sb("plan", [1, 4, PAIRS], I32)

        X = sb("X", [TN, NT, D])
        Hn = [sb(f"Hn{l}", [TN, NT, HW]) for l in range(2)]
        stats = sb("stats", [TN, NT, 6])
        mv = sb("mv", [TN, NT, 2])
        rstd = sb("rstd", [TN, 4, NT])

        rec = [sb(f"rec{b}", [128, T, 4], I32) for b in range(2)]
        G = [sb(f"G{b}", [128, T, GW]) for b in range(2)]
        S = [sb(f"S{b}", [128, T, TN]) for b in range(2)]
        dloc = sb("dloc", [128, 2, T])
        ST = sb("ST", [TN, T, 128])
        SM = sb("SM", [TN, T, 128])
        vT = sb("vT", [T, H, 128])
        junk = sb("junk", [TN, H, GRP * 128])
        mx = sb("mx", [TN, H, NG])
        mc = sb("mc", [TN, H])
        Gs = sb("Gs", [128, T, H * (C + 1)])
        z = sb("z", [128, 4, T, H])
        p = sb("p", [128, T, H])
        M = sb("M", [TN, 2, H])
        nv = sb("nv", [TN, 2, 4])
        mold = sb("mold", [TN, 2, H])
        zn = sb("zn", [TN, 2, H])
        dm = sb("dm", [TN, 2, H])
        scl = sb("scl", [TN, 2, H])
        acc = sb("acc", [TN, 2, H * (C + 1)])
        rs = sb("rs", [TN, 2, 2, H])
        o = sb("o", [TN, 2, D])
        hb = [sb(f"hb{b}", [TN, D]) for b in range(2)]
        hT = [sb(f"hT{b}", [128, TN]) for b in range(2)]
        tstage = [sb(f"tstage{b}", [TN, R * D]) for b in range(2)]

        psT = [ps("psT0"), ps("psT1")]
        psV = [ps("psV0"), ps("psV1")]
        psA = ps("psA")
        psE = ps("psE")
        psF = [ps("psF0"), ps("psF1")]

        s_small, s_W, s_V, s_X = sem("s_small"), sem("s_W"), [sem("s_V0"), sem("s_V1")], sem("s_X")
        s_edges, s_zeroed, s_iota, s_const = sem("s_edges"), sem("s_zeroed"), sem("s_iota"), sem("s_const")
        s_packed, s_records, s_counted, s_counts, s_plan = (
            sem("s_packed"), sem("s_records"), sem("s_counted"), sem("s_counts"), sem("s_plan"))
        s_setup = sem("s_setup")
        s_wext, s_relw = sem("s_wext"), [sem("s_relw0"), sem("s_relw1")]
        s_var, s_rstd = sem("s_var"), sem("s_rstd")
        s_final, s_out = sem("s_final"), sem("s_out")
        s_pool, s_vector = sem("s_pool"), sem("s_vector")

        def per(name, n):
            return [sem(f"{name}{i}") for i in range(n)]

        s_rec = [[sem(f"s_rec{l}{b}") for b in range(2)] for l in range(4)]
        s_rows = [[sem(f"s_rows{l}{b}") for b in range(2)] for l in range(4)]
        s_onehot = per("s_onehot", 4)
        s_summed = per("s_summed", 4)
        s_own = per("s_own", 4)
        s_init = per("s_init", 4)
        s_turned = per("s_turned", 2)
        s_masks = per("s_masks", 2)
        s_vturn = per("s_vturn", 2)
        s_vrow = per("s_vrow", 2)
        s_spread = per("s_spread", 2)
        s_seen = per("s_seen", 2)
        s_nodeval = per("s_nodeval", 2)
        s_edgeval = per("s_edgeval", 2)
        s_expin = per("s_expin", 2)
        s_expout = per("s_expout", 2)
        s_weighed = per("s_weighed", 2)
        s_fin = per("s_fin", 3)
        s_h = per("s_h", 4)
        s_hturn = per("s_hturn", 4)
        s_hcopy = per("s_hcopy", 4)
        s_prod = per("s_prod", 4)
        s_node = per("s_node", 4)
        s_table = [[sem(f"s_table{i}{b}") for b in range(2)] for i in range(4)]

        SEEN0 = 22
        WEIGHED0 = 2 * NG
        SUMMED0 = 2
        NODEC = 2
        NODE0 = 2 * NODEC
        OWN = 10
        HC = [1, 2, 1, 1]
        HT0 = [2, 0, 0, 0]

        block = ctx.enter_context(nc.Block())

        def flat(ap):
            return ap.rearrange("h c -> (h c)")

        def pair_loop(eng, chunk_body, before, after, last=False):
            with eng.Fori(0, PAIRS) as j:
                first = eng.value_load(plan[0:1, 0, bass.ds(j, 1)], min_val=0, max_val=PAIRS * MAXC)
                end = eng.value_load(plan[0:1, 1, bass.ds(j, 1)], min_val=1, max_val=PAIRS * MAXC)
                before(j)
                with eng.Fori(first, end) as g:
                    chunk_body(j, g, first)
                after(j, end)

        @block.sync
        def _(sp):
            sp.wait_ge(s_zeroed, 1)
            n = EFULL * EC
            for t, a in ((dst_all, dst), (src_all, src), (typ_all, etype), (wgt_all, eweight)):
                sp.dma_start(t[0:EFULL, :], a[0:n].rearrange("(p t) -> p t", t=EC)).then_inc(s_edges, 16)
                sp.dma_start(t[EFULL:EFULL + 1, 0:EREST], a[n:E].unsqueeze(0)).then_inc(s_edges, 16)
            sp.dma_start(nxt_all[0:EFULL, :], dst[1:n + 1].rearrange("(p t) -> p t", t=EC)).then_inc(s_edges, 16)
            sp.dma_start(nxt_all[EFULL:EFULL + 1, 0:EREST - 1], dst[n + 1:E].unsqueeze(0)).then_inc(s_edges, 16)
            sp.wait_ge(s_packed, 5)
            sp.dma_start(records[0:128 * EC, :].rearrange("(p t) c -> p t c", t=EC), rec_all[:, :, :]).then_inc(s_records, 16)
            sp.dma_start(records[128 * EC:EPAD, :].rearrange("(p t) c -> p t c", t=PADC), rec_pad[:, :, :]).then_inc(s_records, 16)
            sp.wait_ge(s_records, 32)
            sp.wait_ge(s_plan, 1)

            for l in range(4):
                if l > 0:
                    sp.wait_ge(s_h[l], HC[l] * NT)
                with sp.Fori(0, PAIRS) as j:
                    first = sp.value_load(plan[0:1, 0, bass.ds(j, 1)], min_val=0, max_val=PAIRS * MAXC)
                    end = sp.value_load(plan[0:1, 1, bass.ds(j, 1)], min_val=1, max_val=PAIRS * MAXC)
                    run = [sp.value_load(plan[0:1, 2 + b, bass.ds(j, 1)], min_val=0, max_val=E) for b in range(2)]
                    with sp.Fori(first, end) as g:
                        for b in range(2):
                            start = nc.s_assert_within(run[b] + (g - first) * CH, 0, EPAD - CH, skip_runtime_bounds_check_because="a run starts at E at the latest and has at most MAXC chunks")
                            if l < 2:
                                sp.wait_ge(s_seen[l], g * 20 + (10 * b + 3))
                            else:
                                sp.wait_ge(s_summed[l], g * 2 + (b + 1))
                            sp.dma_start(rec[b][:, :, :],
                                         records[bass.ds(start, CH), :].rearrange("(p t) c -> p t c", t=T)
                                         ).then_inc(s_rec[l][b], 16)
            sp.wait_ge(s_final, PAIRS)
            m = (NT - 1) * TN
            sp.dma_start(out[0:m, :].rearrange("(n p) d -> p n d", p=TN), X[:, 0:NT - 1, :]).then_inc(s_out, 16)
            sp.dma_start(out[m:N, :], X[0:LAST, NT - 1, :]).then_inc(s_out, 16)
            sp.wait_ge(s_out, 32)

        @block.gpsimd
        def _(pool):
            nc.gpsimd.memset(ident[:, :], 0.0).then_inc(s_iota, 1)
            nc.gpsimd.iota(iota_i[:, :], pattern=[[1, TN]], base=0, channel_multiplier=0).then_inc(s_iota, 1)
            nc.gpsimd.iota(base_i[:, :], pattern=[[TN, NT + 1]], base=0, channel_multiplier=0).then_inc(s_iota, 1)
            nc.gpsimd.iota(steps_i[:, :], pattern=[[CH, MAXC - 1]], base=CH, channel_multiplier=0).then_inc(s_iota, 1)
            pool.wait_ge(s_iota, 4)
            nc.gpsimd.affine_select(out=ident[:, :], in_=ident[:, :], compare_op=ALU.not_equal, fill=1.0, base=0,
                                    pattern=[[-1, 128]], channel_multiplier=1).then_inc(s_const, 1)
            pool.wait_ge(s_plan, 1)
            for l in range(4):
                table = gat_rows[l] if l < 2 else rel_rows[l - 2]
                c0 = 0 if l < 2 else 16
                pool.wait_ge(s_table[l][0], 16 * PAIRS + c0)
                pool.wait_ge(s_table[l][1], 16 * PAIRS + c0)
                with pool.Fori(0, PAIRS) as j:
                    first = pool.value_load(plan[0:1, 0, bass.ds(j, 1)], min_val=0, max_val=PAIRS * MAXC)
                    end = pool.value_load(plan[0:1, 1, bass.ds(j, 1)], min_val=1, max_val=PAIRS * MAXC)
                    with pool.Fori(first, end) as g:
                        for b in range(2):
                            if l < 2:
                                pool.wait_ge(s_weighed[l], g * (2 * NG) + (b + 1) * NG)
                            else:
                                pool.wait_ge(s_summed[l], g * 2 + (b + 1))
                            pool.sem_inc(s_pool, 1)
                            pool.wait_ge(s_rec[l][b], g * 16 + 16)
                            pool.sem_inc(s_pool, 1)
                            for t in range(T):
                                col = 0 if l < 2 else 1
                                rows = G[b][:, t, :] if l < 2 else G[b][:, t, 0:D]
                                nc.gpsimd.indirect_dma_start(
                                    rows, None, table,
                                    bass.IndirectOffsetOnAxis(ap=rec[b][:, t, col:col + 1], axis=0)
                                ).then_inc(s_rows[l][b], 16)

        @block.scalar
        def _(act):
            for t, a in ((w1, W1), (w2, W2)):
                act.dma_start(t[:, 0:D], a).then_inc(s_W, 16)
            for i, a in enumerate((b1, b2, c1, c2)):
                act.dma_start(bias[:, i, :], a.partition_broadcast(128)).then_inc(s_small, 16)
            for t, a, d in ((score1, as1, ad1), (score2, as2, ad2)):
                act.dma_start(t[:, 0:2, :].rearrange("p h c -> p (h c)"), flat(a).partition_broadcast(128)).then_inc(s_small, 16)
                act.dma_start(t[:, 2:4, :].rearrange("p h c -> p (h c)"), flat(d).partition_broadcast(128)).then_inc(s_small, 16)
            for i, a in enumerate((comp1, comp2)):
                act.dma_start(comp[:, i, :], flat(a).partition_broadcast(128)).then_inc(s_small, 16)
            m = (NT - 1) * TN
            act.wait_ge(s_zeroed, 2)
            act.dma_start(X[:, 0:NT - 1, :], x[0:m, :].rearrange("(n p) d -> p n d", p=TN)).then_inc(s_X, 16)
            act.dma_start(X[0:LAST, NT - 1, :], x[m:N, :]).then_inc(s_X, 16)
            act.dma_start(V[:, :, :], V1.rearrange("b i o -> i b o")).then_inc(s_V[0], 16)

            def begin_rstd(n, var, work):
                act.wait_ge(s_var, n)
                nc.scalar.activation(work, var, ACT.Ln).then_inc(s_rstd, 1)
                act.wait_ge(s_rstd, 2 * n - 1)
                nc.scalar.activation(work, work, ACT.Exp, scale=-0.5).then_inc(s_rstd, 1)

            def node_pass(i, j):
                rel = i >= 2
                act.wait_ge(s_hturn[i], j * 2 + (2 + HT0[i]))
                for b in range(2):
                    nc.scalar.activation(hT[b][:, :], psF[0][:, b * 128:b * 128 + TN], ACT.Relu).then_inc(s_hcopy[i], 1)
                for b in range(2):
                    act.wait_ge(s_prod[i], j * 2 + (b + 1))
                    if rel:
                        act.wait_ge(s_table[i][b], j * 16 + 16)
                        for k in range(2):
                            nc.scalar.copy(tstage[b][:, k * 512:(k + 1) * 512], psF[k][0:TN, :]).then_inc(s_node[i], 1)
                        act.wait_ge(s_node[i], j * (2 * NODEC) + (NODE0 + NODEC * (b + 1)))
                        act.dma_start(rel_rows[i - 2][bass.ds((j * 2 + b) * (TN * R), TN * R), :].rearrange("(p r) d -> p (r d)", r=R),
                                      tstage[b][:, :]).then_inc(s_table[i][b], 16)
                    else:
                        row_ = Hn[i][:, bass.ds(j * 2 + b, 1), :].rearrange("p n w -> p (n w)")
                        nc.scalar.copy(row_[:, 0:2 * (C + 1)].rearrange("p (h c) -> p h c", h=2)[:, :, 0:C],
                                       psF[b][0:TN, 0:D].rearrange("p (h c) -> p h c", h=2)).then_inc(s_node[i], 1)
                        nc.scalar.copy(row_[:, 2 * (C + 1):HW], psF[b][0:TN, D:D + 4]).then_inc(s_node[i], 1)
                        act.wait_ge(s_node[i], j * (2 * NODEC) + (NODE0 + NODEC * (b + 1)))
                        act.dma_start(gat_rows[i][bass.ds((j * 2 + b) * TN, TN), :], row_[:, 0:GW]).then_inc(s_table[i][b], 16)

            for i in range(4):
                act.sem_inc(s_node[i], NODE0)
                if i >= 2:
                    for b in range(2):
                        act.sem_inc(s_table[i][b], 16)
            for l in range(2):
                act.sem_inc(s_masks[l], 2)

            begin_rstd(1, rstd[:, 0, :], rstd[:, 1, :])
            with act.Fori(0, PAIRS) as j:
                node_pass(0, j)
            act.wait_ge(s_plan, 1)

            for l in range(2):
                if l == 1:
                    act.wait_ge(s_relw[0], 1)
                    act.dma_start(V[:, :, :], V2.rearrange("b i o -> i b o")).then_inc(s_V[1], 16)

                def chunk(j, g, first):
                    for b in range(2):
                        for k, t0, t1 in groups():
                            act.wait_ge(s_turned[l], g * (2 * NG) + (b * NG + k + 1))
                            if k == 0:
                                act.wait_ge(s_edgeval[l], g * 2 + (b + 1))
                                act.wait_ge(s_seen[l], g * 20 + (SEEN0 + 10 * b))
                            src_ = psT[(b * NG + k) % 2][0:TN, 0:(t1 - t0) * 128].rearrange("p (t e) -> p t e", e=128)
                            nc.scalar.copy(ST[:, t0:t1, :], src_)
                            nc.scalar.activation(SM[:, t0:t1, :], src_, ACT.Copy, bias=-FAR, scale=FAR).then_inc(s_masks[l], 1)
                        act.wait_ge(s_vturn[l], g * 2 + (b + 1))
                        nc.scalar.copy(vT[:, :, :].rearrange("p h e -> p (h e)"), psE[0:T, 128:128 + H * 128]).then_inc(s_vrow[l], 1)
                        act.wait_ge(s_expin[l], g * 4 + (2 * b + 1))
                        nc.scalar.activation(scl[:, b, :], dm[:, b, :], ACT.Exp).then_inc(s_expout[l], 1)
                        act.wait_ge(s_expin[l], g * 4 + (2 * b + 2))
                        nc.scalar.activation(p[:, :, :], z[:, 3, :, :], ACT.Exp).then_inc(s_expout[l], 1)

                def after(j, end):
                    if l == 1:
                        act.wait_ge(s_var, j + 2)
                        nc.scalar.activation(rstd[:, 1, 0:2], rstd[:, 0, 0:2], ACT.Ln).then_inc(s_rstd, 1)
                        act.wait_ge(s_rstd, j * 2 + 3)
                        nc.scalar.activation(rstd[:, 1, 0:2], rstd[:, 1, 0:2], ACT.Exp, scale=-0.5).then_inc(s_rstd, 1)
                    node_pass(l + 1, j)

                pair_loop(act, chunk, lambda j: None, after)
            with act.Fori(0, PAIRS) as j:
                node_pass(3, j)

        @block.tensor
        def _(pe):
            def node_pass(i, j):
                pe.wait_ge(s_node[i], j * (2 * NODEC) + NODE0)
                for b in range(2):
                    pe.wait_ge(s_h[i], j * (2 * HC[i]) + HC[i] * (b + 1))
                    nc.tensor.transpose(psF[0][:, b * 128:b * 128 + TN], hb[b][:, :], ident[0:TN, 0:TN]).then_inc(s_hturn[i], 1)
                for b in range(2):
                    pe.wait_ge(s_hcopy[i], j * 2 + 2)
                    if i >= 2:
                        if b == 1:
                            pe.wait_ge(s_node[i], j * (2 * NODEC) + (NODE0 + NODEC))
                        for k in range(2):
                            mm = nc.tensor.matmul(psF[k][0:TN, :], hT[b][:, :],
                                                  rel_w[i - 2][:, 4 * k:4 * k + 4, :].rearrange("p r d -> p (r d)"),
                                                  start=True, stop=True)
                        mm.then_inc(s_prod[i], 1)
                    else:
                        nc.tensor.matmul(psF[b][0:TN, 0:D + 4], hT[b][:, :], (w1, w2)[i][:, :],
                                         start=True, stop=True).then_inc(s_prod[i], 1)

            pe.sem_inc(s_hturn[0], HT0[0])
            pe.sem_inc(s_edgeval[0], 1)
            pe.sem_inc(s_edgeval[1], 1)
            for l in range(4):
                pe.sem_inc(s_summed[l], SUMMED0)
            pe.wait_ge(s_counted, 1)
            nc.tensor.matmul(psE[0:1, 0:NT + 2], ones[:, 0:1], counts[:, :], start=True, stop=True).then_inc(s_counts, 1)
            pe.wait_ge(s_const, 1)
            pe.wait_ge(s_wext, 1)
            with pe.Fori(0, PAIRS) as j:
                node_pass(0, j)
            pe.wait_ge(s_plan, 1)

            for l in range(2):
                if l == 1:
                    pe.wait_ge(s_relw[0], 1)

                def chunk(j, g, first):
                    for b in range(2):
                        pe.wait_ge(s_onehot[l], g * 2 + (b + 1))
                        for k, t0, t1 in groups():
                            pe.wait_ge(s_masks[l], g * (2 * NG) + (b * NG + k + 1))
                            for t in range(t0, t1):
                                mm = nc.tensor.transpose(psT[(b * NG + k) % 2][0:TN, (t - t0) * 128:(t - t0 + 1) * 128],
                                                         S[b][:, t, :], ident[:, :])
                            mm.then_inc(s_turned[l], 1)
                        pe.wait_ge(s_rows[l][b], g * (16 * T) + 16 * T)
                        for h in range(H):
                            mm = nc.tensor.transpose(psE[0:T, (h + 1) * 128:(h + 2) * 128], G[b][:, :, 2 * (C + 1) + h], ident[:, :])
                        mm.then_inc(s_vturn[l], 1)
                        pe.wait_ge(s_vrow[l], g * 2 + (b + 1))
                        for k, t0, t1 in groups():
                            for h in range(H):
                                pe.wait_ge(s_seen[l], g * 20 + (10 * b + 2 * k + h - 1 + SEEN0))
                                for t in range(t0, t1):
                                    mm = nc.tensor.matmul(psV[h][0:TN, (t - t0) * 128:(t - t0 + 1) * 128],
                                                          pick[:, t, :], vT[:, h, :], start=True, stop=True)
                                mm.then_inc(s_spread[l], 1)
                        pe.wait_ge(s_nodeval[l], g * 2 + (b + 1))
                        for t in range(T):
                            mm = nc.tensor.matmul(psE[:, 4 * t:4 * t + 4], ST[:, t, :], nv[:, b, :], start=True, stop=True)
                        mm.then_inc(s_edgeval[l], 1)
                        for k, t0, t1 in groups():
                            pe.wait_ge(s_weighed[l], g * (2 * NG) + (b * NG + k + 1 + WEIGHED0))
                            for t in range(t0, t1):
                                mm = nc.tensor.matmul(psA[0:TN, 0:H * (C + 1)], S[b][:, t, :], Gs[:, t, :],
                                                      start=(t == 0), stop=(t == T - 1))
                        mm.then_inc(s_summed[l], 1)

                pair_loop(pe, chunk, lambda j: None, lambda j, end: node_pass(l + 1, j))

            pe.wait_ge(s_relw[1], 1)
            for l in range(2, 4):
                def chunk(j, g, first):
                    for b in range(2):
                        pe.wait_ge(s_onehot[l], g * 2 + (b + 1))
                        pe.wait_ge(s_rows[l][b], g * (16 * T) + 16 * T)
                        for t in range(T):
                            mm = nc.tensor.matmul((psA, psE)[b][0:TN, 0:D], S[b][:, t, :], G[b][:, t, 0:D],
                                                  start=(t == 0), stop=(t == T - 1))
                        mm.then_inc(s_summed[l], 1)

                pair_loop(pe, chunk, lambda j: None, lambda j, end: node_pass(l + 1, j) if l == 2 else None)

        @block.vector
        def _(dve):
            steps_done = [0]

            def link(ins):
                steps_done[0] += 1
                ins.then_inc(s_setup, 1)
                dve.wait_ge(s_setup, steps_done[0])

            nc.vector.memset(dst_all[:, :], 65536)
            nc.vector.memset(nxt_all[:, :], 65536)
            nc.vector.memset(src_all[:, :], 0)
            nc.vector.memset(typ_all[:, :], 0)
            nc.vector.memset(wgt_all[:, :], 0.0).then_inc(s_zeroed, 1)
            nc.vector.memset(X[:, NT - 1, :], 0.0).then_inc(s_zeroed, 1)
            nc.vector.memset(ones[:, :], 1.0)
            nc.vector.memset(counts[:, 0:1], 0.0)
            nc.vector.memset(rec_pad[:, :, :], 0)
            nc.vector.memset(Hn[0][:, :, :], 1.0)
            link(nc.vector.memset(Hn[1][:, :, :], 1.0))
            dve.wait_ge(s_iota, 4)
            nc.vector.tensor_copy(iota[:, :], iota_i[:, :])
            nc.vector.tensor_copy(base[:, :], base_i[:, :])
            nc.vector.tensor_copy(steps[:, :], steps_i[:, :])
            for l in range(2):
                dve.sem_inc(s_seen[l], SEEN0)
                dve.sem_inc(s_weighed[l], WEIGHED0)

            def newton(v, y, a):
                yield nc.vector.tensor_tensor(a, y, y, ALU.mult)
                yield nc.vector.tensor_tensor(a, a, v, ALU.mult)
                yield nc.vector.tensor_scalar(a, a, -0.5, 1.5, ALU.mult, ALU.add)
                yield nc.vector.tensor_tensor(y, y, a, ALU.mult)

            dve.wait_ge(s_W, 32)
            dve.wait_ge(s_small, 16 * 10)
            for w, sc in ((w1, score1), (w2, score2)):
                for i in range(2):
                    link(nc.vector.tensor_tensor(prod[:, :], w[:, 0:D], sc[:, 2 * i:2 * i + 2, :].rearrange("p h c -> p (h c)"), ALU.mult))
                    ins = nc.vector.tensor_reduce(w[:, D + 2 * i:D + 2 * i + 2], prod[:, :].rearrange("p (h c) -> p h c", h=2), AX, ALU.add)
                    link(ins)
            dve.sem_inc(s_wext, 1)

            dve.wait_ge(s_X, 32)
            for n in range(NT):
                ins = nc.vector.bn_stats(stats[:, n, :], X[:, n, :])
            link(ins)
            for n in range(NT):
                ins = nc.vector.bn_aggr(mv[:, n, :], stats[:, n, :])
            link(ins)
            nc.vector.tensor_scalar(rstd[:, 0, :], mv[:, :, 1], EPS_LN, None, ALU.add).then_inc(s_var, 1)

            dve.wait_ge(s_edges, 16 * 10)
            nc.vector.tensor_copy(dst_f[:, :], dst_all[:, :])
            link(nc.vector.tensor_copy(nxt_f[:, :], nxt_all[:, :]))
            nc.vector.tensor_copy(rec_all[:, :, 0], src_all[:, :]).then_inc(s_packed, 1)
            nc.vector.scalar_tensor_tensor(out=rec_all[:, :, 1], in0=src_all[:, :], scalar=float(R), in1=typ_all[:, :],
                                           op0=ALU.mult, op1=ALU.add).then_inc(s_packed, 1)
            nc.vector.tensor_copy(rec_all[:, :, 2].bitcast(F32), dst_f[:, :]).then_inc(s_packed, 1)
            nc.vector.tensor_copy(rec_all[:, :, 3].bitcast(F32), wgt_all[:, :]).then_inc(s_packed, 1)
            nc.vector.memset(rec_pad[:, :, 2].bitcast(F32), 65536.0).then_inc(s_packed, 1)
            for k in range(1, NT + 1):
                link(nc.vector.tensor_scalar(scratch[:, :], dst_f[:, :], float(k * TN), None, ALU.is_lt, ALU.add,
                                             accum_out=counts[:, k:k + 1]))
            link(nc.vector.tensor_tensor(scratch[:, :], nxt_f[:, :], dst_f[:, :], ALU.is_lt))
            nc.vector.tensor_reduce(counts[:, NT + 1:NT + 2], scratch[:, :], AX, ALU.add).then_inc(s_counted, 1)

            dve.wait_ge(s_counts, 1)
            cnt, flag, lo, hi, size, nch, endr = (row[:, i, :] for i in range(7))
            link(nc.vector.tensor_copy(cnt, psE[0:1, 0:NT + 2]))
            link(nc.vector.tensor_scalar(flag[:, 0:1], cnt[:, NT + 1:NT + 2], 1.0, None, ALU.min))
            nc.vector.tensor_scalar(flag[:, 1:2], flag[:, 0:1], -1.0, 1.0, ALU.mult, ALU.add)
            link(nc.vector.tensor_scalar(flag[:, 2:3], flag[:, 0:1], float(E), None, ALU.mult))
            link(nc.vector.tensor_scalar(lo[:, 0:NT], cnt[:, 0:NT], flag[:, 1:2], None, ALU.mult))
            link(nc.vector.tensor_scalar(hi[:, 0:NT], cnt[:, 1:NT + 1], flag[:, 1:2], flag[:, 2:3], ALU.mult, ALU.add))
            link(nc.vector.tensor_tensor(size[:, 0:NT], hi[:, 0:NT], lo[:, 0:NT], ALU.subtract))
            pairs = size[:, 0:NT].rearrange("o (j b) -> o j b", b=2)
            link(nc.vector.tensor_tensor(hi[:, 0:PAIRS], pairs[:, :, 0], pairs[:, :, 1], ALU.max))
            link(nc.vector.tensor_tensor(over[:, :, :], hi[:, 0:PAIRS].unsqueeze(2).to_broadcast([1, PAIRS, MAXC - 1]),
                                         steps[:, :].unsqueeze(1).to_broadcast([1, PAIRS, MAXC - 1]), ALU.is_gt))
            link(nc.vector.tensor_reduce(nch[:, 0:PAIRS], over[:, :, :], AX, ALU.add))
            link(nc.vector.tensor_scalar(nch[:, 0:PAIRS], nch[:, 0:PAIRS], 1.0, None, ALU.add))
            link(nc.vector.tensor_tensor_scan(endr[:, 0:PAIRS], ones[0:1, 0:PAIRS], nch[:, 0:PAIRS], 0.0, ALU.mult, ALU.add))
            link(nc.vector.tensor_tensor(size[:, 0:PAIRS], endr[:, 0:PAIRS], nch[:, 0:PAIRS], ALU.subtract))
            runs = lo[:, 0:NT].rearrange("o (j b) -> o j b", b=2)
            nc.vector.tensor_copy(plan[:, 0, :], size[:, 0:PAIRS])
            nc.vector.tensor_copy(plan[:, 1, :], endr[:, 0:PAIRS])
            nc.vector.tensor_copy(plan[:, 2, :], runs[:, :, 0])
            nc.vector.tensor_copy(plan[:, 3, :], runs[:, :, 1]).then_inc(s_plan, 1)

            dve.wait_ge(s_rstd, 2)
            for ins in newton(rstd[:, 0, :], rstd[:, 1, :], rstd[:, 2, :]):
                link(ins)
            with dve.Fori(0, PAIRS) as j:
                for b in range(2):
                    n = j * 2 + b
                    dve.wait_ge(s_hturn[0], n + 1)
                    nc.vector.tensor_scalar(hb[b][:, :], X[:, bass.ds(n, 1), :].rearrange("p n d -> p (n d)"),
                                            mv[:, bass.ds(n, 1), 0], rstd[:, 1, bass.ds(n, 1)],
                                            ALU.subtract, ALU.mult).then_inc(s_h[0], 1)
            dve.wait_ge(s_const, 1)
            link(nc.vector.tensor_copy(pick[:, :, :], ident[0:T, 0:T].unsqueeze(2).to_broadcast([T, T, TN])))
            dve.wait_ge(s_plan, 1)

            def relation_weights(i):
                dve.wait_ge(s_V[i], 16)
                for b in range(R):
                    for r in range(R):
                        c = comp[:, i, r * R + b:r * R + b + 1]
                        if b == 0:
                            ins = nc.vector.tensor_scalar(rel_w[i][:, r, :], V[:, b, :], c, None, ALU.mult)
                        else:
                            ins = nc.vector.scalar_tensor_tensor(out=rel_w[i][:, r, :], in0=V[:, b, :], scalar=c,
                                                                 in1=rel_w[i][:, r, :], op0=ALU.mult, op1=ALU.add)
                    if b < R - 1:
                        link(ins)
                ins.then_inc(s_relw[i], 1)

            def recs(b, c):
                return rec[b][:, :, c].bitcast(F32)

            for l in range(2):
                relation_weights(l)
                dve.wait_ge(s_node[l], NODEC * NT + NODE0)
                seen, own = s_seen[l], s_own[l]

                def before(j):
                    for b in range(2):
                        node = Hn[l][:, bass.ds(j * 2 + b, 1), :].rearrange("p n w -> p (n w)")
                        nc.vector.tensor_copy(M[:, b, :], node[:, 130:132])
                        nc.vector.tensor_copy(nv[:, b, 0:2], node[:, 132:134])
                        nc.vector.tensor_copy(acc[:, b, :], node[:, 0:130])
                        nc.vector.tensor_tensor(zn[:, b, :], node[:, 130:132], node[:, 132:134], ALU.add).then_inc(s_init[l], 1)
                        dve.wait_ge(s_init[l], j * 4 + (2 * b + 1))
                        nc.vector.scalar_tensor_tensor(out=nv[:, b, 2:4], in0=zn[:, b, :], scalar=SLOPE, in1=zn[:, b, :],
                                                       op0=ALU.mult, op1=ALU.max).then_inc(s_init[l], 1)
                    dve.wait_ge(s_init[l], j * 4 + 4)
                    dve.sem_inc(s_vector, 1)

                def chunk(j, g, first):
                    for b in range(2):
                        def step(k):
                            dve.wait_ge(own, g * (2 * OWN) + (b * OWN + k))
                        dve.wait_ge(s_rec[l][b], g * 16 + 16)
                        nc.vector.tensor_scalar(dloc[:, b, :], recs(b, 2), base[:, bass.ds(j * 2 + b, 1)], None,
                                                ALU.subtract).then_inc(own, 1)
                        step(1)
                        nc.vector.tensor_tensor(S[b][:, :, :], iota[:, :].unsqueeze(1).to_broadcast([128, T, TN]),
                                                dloc[:, b, :].unsqueeze(2).to_broadcast([128, T, TN]),
                                                ALU.is_equal).then_inc(s_onehot[l], 1)
                        for k, t0, t1 in groups():
                            for h in range(H):
                                if h == 0:
                                    dve.wait_ge(s_masks[l], g * (2 * NG) + (b * NG + k + 3))
                                    dve.sem_inc(s_vector, 1)
                                dve.wait_ge(s_spread[l], g * 20 + (10 * b + 2 * k + h + 1))
                                dve.sem_inc(s_vector, 1)
                                w = (t1 - t0) * 128
                                nc.vector.tensor_tensor_reduce(
                                    out=junk[:, h, 0:w], in0=psV[h][0:TN, 0:w], in1=SM[:, t0:t1, :].rearrange("p t e -> p (t e)"),
                                    scale=1.0, scalar=-FAR, op0=ALU.add, op1=ALU.max, accum_out=mx[:, h, k:k + 1]).then_inc(seen, 1)
                        dve.wait_ge(seen, g * 20 + (10 * b + 10 + SEEN0))
                        nc.vector.tensor_reduce(mc[:, :], mx[:, :, :], AX, ALU.max).then_inc(own, 1)
                        step(2)
                        nc.vector.tensor_tensor(M[:, b, :], M[:, b, :], mc[:, :], ALU.max).then_inc(own, 1)
                        nc.vector.tensor_copy(mold[:, b, :], nv[:, b, 2:4]).then_inc(own, 1)
                        step(4)
                        nc.vector.tensor_tensor(zn[:, b, :], M[:, b, :], nv[:, b, 0:2], ALU.add).then_inc(own, 1)
                        step(5)
                        nc.vector.scalar_tensor_tensor(out=nv[:, b, 2:4], in0=zn[:, b, :], scalar=SLOPE, in1=zn[:, b, :],
                                                       op0=ALU.mult, op1=ALU.max).then_inc(s_nodeval[l], 1)
                        dve.wait_ge(s_nodeval[l], g * 2 + (b + 1))
                        nc.vector.tensor_tensor(dm[:, b, :], mold[:, b, :], nv[:, b, 2:4], ALU.subtract).then_inc(s_expin[l], 1)
                        at = psE[:, 0:4 * T].rearrange("p (t v) -> p t v", v=4)
                        dve.wait_ge(s_edgeval[l], g * 2 + (b + 2))
                        nc.vector.tensor_tensor(z[:, 0, :, :], at[:, :, 0:2], G[b][:, :, 130:132], ALU.add).then_inc(own, 1)
                        step(6)
                        nc.vector.scalar_tensor_tensor(out=z[:, 1, :, :], in0=z[:, 0, :, :], scalar=SLOPE, in1=z[:, 0, :, :],
                                                       op0=ALU.mult, op1=ALU.max).then_inc(own, 1)
                        step(7)
                        nc.vector.tensor_tensor(z[:, 2, :, :], z[:, 1, :, :], at[:, :, 2:4], ALU.subtract).then_inc(own, 1)
                        step(8)
                        nc.vector.tensor_scalar(z[:, 3, :, :], z[:, 2, :, :], 0.0, None, ALU.min).then_inc(s_expin[l], 1)
                        dve.wait_ge(s_expout[l], g * 4 + (2 * b + 2))
                        for k, t0, t1 in groups():
                            nc.vector.tensor_tensor(
                                Gs[:, t0:t1, :].rearrange("p t (h c) -> p t h c", h=H),
                                G[b][:, t0:t1, 0:130].rearrange("p t (h c) -> p t h c", h=H),
                                p[:, t0:t1, :].unsqueeze(3).to_broadcast([128, t1 - t0, H, C + 1]),
                                ALU.mult).then_inc(s_weighed[l], 1)
                        dve.wait_ge(s_summed[l], g * 2 + (b + 1 + SUMMED0))
                        for h in range(H):
                            c0, c1_ = h * (C + 1), (h + 1) * (C + 1)
                            nc.vector.scalar_tensor_tensor(out=acc[:, b, c0:c1_], in0=acc[:, b, c0:c1_], scalar=scl[:, b, h:h + 1],
                                                           in1=psA[0:TN, c0:c1_], op0=ALU.mult, op1=ALU.add).then_inc(own, 1)

                def after(j, end):
                    F = 2 if l == 0 else 10
                    done = [0]

                    def fin(ins, wait=True):
                        done[0] += 1
                        ins.then_inc(s_fin[l], 1)
                        if wait:
                            dve.wait_ge(s_fin[l], j * F + done[0])
                            dve.sem_inc(s_vector, 1)
                    dve.wait_ge(own, end * (2 * OWN))
                    sums = acc[:, :, :].rearrange("p b (h c) -> p (b h) c", c=C + 1)
                    den = rs[:, 0, :, :].rearrange("p b h -> p (b h)")
                    inv = rs[:, 1, :, :].rearrange("p b h -> p (b h)")
                    fin(nc.vector.tensor_scalar(den.unsqueeze(2), sums[:, :, C:C + 1], 1e-16, None, ALU.add))
                    fin(nc.vector.reciprocal(inv, den))
                    for b in range(2):
                        for h in range(H):
                            target = hb[b] if l == 0 else o[:, b, :]
                            ins = nc.vector.scalar_tensor_tensor(
                                out=target[:, h * C:(h + 1) * C], in0=acc[:, b, h * (C + 1):h * (C + 1) + C],
                                scalar=rs[:, 1, b, h:h + 1], in1=bias[0:TN, l, h * C:(h + 1) * C], op0=ALU.mult, op1=ALU.add)
                            if l == 0:
                                ins.then_inc(s_h[1], 1)
                    if l == 0:
                        dve.wait_ge(s_h[1], j * (2 * HC[1]) + 2 * HC[1])
                        dve.sem_inc(s_vector, 1)
                        return
                    fin(ins)
                    for b in range(2):
                        xn = X[:, bass.ds(j * 2 + b, 1), :].rearrange("p n d -> p (n d)")
                        ins = nc.vector.scalar_tensor_tensor(out=xn, in0=o[:, b, :], scalar=0.0, in1=xn, op0=ALU.max, op1=ALU.add)
                    fin(ins)
                    for b in range(2):
                        ins = nc.vector.bn_stats(stats[:, b, :], X[:, bass.ds(j * 2 + b, 1), :].rearrange("p n d -> p (n d)"))
                    fin(ins)
                    for b in range(2):
                        ins = nc.vector.bn_aggr(mv[:, b, :], stats[:, b, :])
                    fin(ins)
                    nc.vector.tensor_scalar(rstd[:, 0, 0:2], mv[:, 0:2, 1], EPS_LN, None, ALU.add).then_inc(s_var, 1)
                    dve.wait_ge(s_rstd, j * 2 + 4)
                    for ins in newton(rstd[:, 0, 0:2], rstd[:, 1, 0:2], rstd[:, 2, 0:2]):
                        fin(ins)
                    for b in range(2):
                        nc.vector.tensor_scalar(hb[b][:, :], X[:, bass.ds(j * 2 + b, 1), :].rearrange("p n d -> p (n d)"),
                                                mv[:, b, 0:1], rstd[:, 1, b:b + 1], ALU.subtract, ALU.mult).then_inc(s_h[2], 1)
                    dve.wait_ge(s_h[2], j * 2 + 2)
                    dve.sem_inc(s_vector, 1)

                pair_loop(dve, chunk, before, after)

            for l in range(2, 4):
                def before(j):
                    for b in range(2):
                        if l == 2:
                            nc.vector.tensor_copy(acc[:, b, 0:D], bias[0:TN, l, :]).then_inc(s_init[l], 1)
                        else:
                            nc.vector.tensor_tensor(acc[:, b, 0:D], X[:, bass.ds(j * 2 + b, 1), :].rearrange("p n d -> p (n d)"),
                                                    bias[0:TN, l, :], ALU.add).then_inc(s_init[l], 1)
                    dve.wait_ge(s_init[l], j * 2 + 2)
                    dve.sem_inc(s_vector, 1)

                def chunk(j, g, first):
                    for b in range(2):
                        dve.wait_ge(s_rec[l][b], g * 16 + 16)
                        nc.vector.tensor_scalar(dloc[:, b, :], recs(b, 2), base[:, bass.ds(j * 2 + b, 1)], None,
                                                ALU.subtract).then_inc(s_own[l], 1)
                        dve.wait_ge(s_own[l], g * 4 + (2 * b + 1))
                        for t in range(T):
                            ins = nc.vector.tensor_scalar(S[b][:, t, :], iota[:, :], dloc[:, b, t:t + 1], recs(b, 3)[:, t:t + 1],
                                                          ALU.is_equal, ALU.mult)
                        ins.then_inc(s_onehot[l], 1)
                        dve.wait_ge(s_summed[l], g * 2 + (b + 1 + SUMMED0))
                        nc.vector.tensor_tensor(acc[:, b, 0:D], acc[:, b, 0:D], (psA, psE)[b][0:TN, 0:D], ALU.add).then_inc(s_own[l], 1)

                def after(j, end):
                    dve.wait_ge(s_own[l], end * 4)
                    dve.sem_inc(s_vector, 1)
                    for b in range(2):
                        if l == 2:
                            nc.vector.tensor_copy(hb[b][:, :], acc[:, b, 0:D]).then_inc(s_h[3], 1)
                        else:
                            ins = nc.vector.tensor_copy(X[:, bass.ds(j * 2 + b, 1), :].rearrange("p n d -> p (n d)"), acc[:, b, 0:D])
                    if l == 3:
                        ins.then_inc(s_final, 1)
                    dve.wait_ge(s_h[3] if l == 2 else s_final, j * 2 + 2 if l == 2 else j + 1)
                    dve.sem_inc(s_vector, 1)

                pair_loop(dve, chunk, before, after)


_INS = ["x", "src", "dst", "edge_type_8", "edge_weight", "L0_gnn_W1", "L0_gnn_a_src1", "L0_gnn_a_dst1", "L0_gnn_b1",
        "L0_gnn_W2", "L0_gnn_a_src2", "L0_gnn_a_dst2", "L0_gnn_b2", "L1_gnn_comp1", "L1_gnn_V1", "L1_gnn_bias1",
        "L1_gnn_comp2", "L1_gnn_V2", "L1_gnn_bias2"]


def kernel(**inputs):
    import numpy as _np
    import concourse.bacc as _bacc
    from concourse import mybir as _mybir
    from concourse.bass_utils import run_bass_kernel_spmd as _run

    nc = _bacc.Bacc("TRN2", target_bir_lowering=False, num_devices=1)
    arrays, args = {}, []
    for name in _INS:
        a = _np.ascontiguousarray(inputs[name])
        arrays[f"in_{name}_dram"] = a
        args.append(nc.dram_tensor(f"in_{name}_dram", a.shape, _mybir.dt.from_np(a.dtype), kind="ExternalInput").ap())
    out = nc.dram_tensor("out_0_dram", (N, D), _mybir.dt.float32, kind="ExternalOutput").ap()
    build(nc, *args, out)
    r = _run(nc, [arrays], core_ids=[0])
    return r.results[0]["out_0_dram"]
```

```python
from contextlib import ExitStack

import concourse.bass as bass
from concourse import mybir

F32 = mybir.dt.float32
I32 = mybir.dt.int32
BF16 = mybir.dt.bfloat16
ALU = mybir.AluOpType
ACT = mybir.ActivationFunctionType
AX = mybir.AxisListType.X

N = 3125
E = 53125
D = 128
H = 2
C = D // H
R = 8
TN = 121
NT = -(-N // TN)
PAIRS = NT // 2
LAST = N - (NT - 1) * TN
T = 17
CH = 128 * T
MAXC = -(-E // CH)
EC = -(-E // 128)
EFULL = E // EC
EREST = E - EFULL * EC
PADC = 425
EPAD = 128 * (EC + PADC)
GW = 132
HW = 134
GRP = 4
NG = -(-T // GRP)
EPS_LN = 1e-5
SLOPE = 0.2
FAR = 1e30
PARTS = 3

assert NT == 2 * PAIRS and EPAD >= E + MAXC * CH and 0 < EREST < EC


def groups():
    return [(k, k * GRP, min(T, (k + 1) * GRP)) for k in range(NG)]


def spreads():
    return [(2 * k + h, h, t0, t1) for k, t0, t1 in groups() for h in range(H)]


def build(nc, x, src, dst, etype, eweight, W1, as1, ad1, b1, W2, as2, ad2, b2,
          comp1, V1, c1, comp2, V2, c2, out):
    with ExitStack() as ctx:
        def sb(name, shape, dt=F32):
            return ctx.enter_context(nc.sbuf_tensor(name, shape, dt))

        def ps(name):
            return ctx.enter_context(nc.psum_tensor(name, [128, 512], F32))

        def sem(name):
            return ctx.enter_context(nc.semaphore(name))

        records = nc.dram_tensor("records", (EPAD, 4), I32).ap()
        gat_rows = [nc.dram_tensor(f"gat_rows{l}", (NT * TN, GW), F32).ap() for l in range(2)]
        rel_rows = [nc.dram_tensor(f"rel_rows{l}", (NT * TN * R, D), F32).ap() for l in range(2)]

        ident = sb("ident", [128, 128])
        ident16 = sb("ident16", [128, 128], BF16)
        ones = sb("ones", [128, 128])
        pick = sb("pick", [PARTS * T, T, TN], BF16)
        iota_i = sb("iota_i", [128, TN], I32)
        iota = sb("iota", [128, TN])
        base_i = sb("base_i", [128, NT + 1], I32)
        base = sb("base", [128, NT + 1])
        w1 = sb("w1", [128, D + 4])
        w2 = sb("w2", [128, D + 4])
        score1 = sb("score1", [128, 4, C])
        score2 = sb("score2", [128, 4, C])
        prod = sb("prod", [128, D])
        bias = sb("bias", [128, 4, D])
        comp = sb("comp", [128, 2, R * R])
        V = sb("V", [128, R, D])
        rel_w = [sb(f"rel_w{l}", [128, R, D]) for l in range(2)]

        src_all = sb("src_all", [128, EC], I32)
        dst_all = sb("dst_all", [128, EC], I32)
        nxt_all = sb("nxt_all", [128, EC], I32)
        typ_all = sb("typ_all", [128, EC], I32)
        wgt_all = sb("wgt_all", [128, EC])
        dst_f = sb("dst_f", [128, EC])
        nxt_f = sb("nxt_f", [128, EC])
        scratch = sb("scratch", [128, EC])
        rec_all = sb("rec_all", [128, EC, 4], I32)
        rec_pad = sb("rec_pad", [128, PADC, 4], I32)
        counts = sb("counts", [128, NT + 2])
        row = sb("row", [1, 8, NT + 2])
        steps_i = sb("steps_i", [1, MAXC - 1], I32)
        steps = sb("steps", [1, MAXC - 1])
        over = sb("over", [1, PAIRS, MAXC - 1])
        plan = sb("plan", [1, 6, PAIRS], I32)

        X = sb("X", [TN, NT, D])
        Hn = [sb(f"Hn{l}", [TN, NT, HW]) for l in range(2)]
        stats = sb("stats", [TN, NT, 6])
        mv = sb("mv", [TN, NT, 2])
        rstd = sb("rstd", [TN, 4, NT])

        rec = [sb(f"rec{b}", [128, T, 4], I32) for b in range(2)]
        G = [sb(f"G{b}", [128, T, GW]) for b in range(2)]
        S = [sb(f"S{b}", [128, T, TN]) for b in range(2)]
        dloc = sb("dloc", [128, 2, T])
        ST = [sb(f"ST{b}", [TN, T, 128], BF16) for b in range(2)]
        SM = [sb(f"SM{b}", [TN, T, 128], BF16) for b in range(2)]
        vp = sb("vp", [128, H, PARTS, T], BF16)
        vr = sb("vr", [128, H, T])
        vT = sb("vT", [PARTS * T, H, 128], BF16)
        nvp = sb("nvp", [TN, PARTS, 4], BF16)
        nvr = sb("nvr", [TN, 4])
        ev = sb("ev", [128, T, 4])
        junk = sb("junk", [TN, 3, GRP * 128])
        mx = sb("mx", [TN, H, NG])
        mc = sb("mc", [TN, H])
        Gs = sb("Gs", [128, T, H * (C + 1)])
        z = sb("z", [128, 4, T, H])
        p = sb("p", [128, T, H])
        M = sb("M", [TN, 2, H])
        nv = sb("nv", [TN, 2, 4])
        mold = sb("mold", [TN, 2, H])
        zn = sb("zn", [TN, 2, H])
        dm = sb("dm", [TN, 2, H])
        scl = sb("scl", [TN, 2, H])
        acc = sb("acc", [TN, 2, H * (C + 1)])
        rs = sb("rs", [TN, 2, 2, H])
        o = sb("o", [TN, 2, D])
        hb = [sb(f"hb{b}", [TN, D]) for b in range(2)]
        hT = [sb(f"hT{b}", [128, TN]) for b in range(2)]
        tstage = [sb(f"tstage{b}", [TN, R * D]) for b in range(2)]

        psT = [ps("psT0"), ps("psT1")]
        psV = [ps(f"psV{i}") for i in range(3)]
        psA = ps("psA")
        psE = psA[:, 130:130 + 12 * T]
        psF = [ps("psF0"), ps("psF1")]
        vturned = psF[1][0:PARTS * T, 384:384 + H * 64].bitcast(BF16)

        s_small, s_W, s_V, s_X = sem("s_small"), sem("s_W"), [sem("s_V0"), sem("s_V1")], sem("s_X")
        s_edges, s_zeroed, s_iota, s_const = sem("s_edges"), sem("s_zeroed"), sem("s_iota"), sem("s_const")
        s_packed, s_records, s_counted, s_counts, s_plan = (
            sem("s_packed"), sem("s_records"), sem("s_counted"), sem("s_counts"), sem("s_plan"))
        s_setup = sem("s_setup")
        s_wext, s_relw = sem("s_wext"), [sem("s_relw0"), sem("s_relw1")]
        s_ident16 = sem("s_ident16")
        s_final, s_out = sem("s_final"), sem("s_out")
        s_pool, s_vector, s_tensor = sem("s_pool"), sem("s_vector"), sem("s_tensor")

        def per(name, n):
            return [sem(f"{name}{i}") for i in range(n)]

        def per_layer(name, n=4):
            first = sem(f"{name}01")
            return ([first, first] + [sem(f"{name}{l}") for l in range(2, 4)])[0:n]

        s_rec = [list(x) for x in zip(per_layer("s_rec_a"), per_layer("s_rec_b"))]
        s_rows = [list(x) for x in zip(per_layer("s_rows_a"), per_layer("s_rows_b"))]
        s_onehot = per_layer("s_onehot")
        s_summed = per_layer("s_summed")
        s_own = per_layer("s_own")
        s_init = per("s_init", 4)
        s_turned = sem("s_turned")
        s_masks = sem("s_masks")
        s_vparts = sem("s_vparts")
        s_vturn = sem("s_vturn")
        s_vrow = sem("s_vrow")
        s_spread = sem("s_spread")
        s_seen = sem("s_seen")
        s_nodeval = sem("s_nodeval")
        s_edgeval = sem("s_edgeval")
        s_expin = sem("s_expin")
        s_expout = sem("s_expout")
        s_weighed = sem("s_weighed")
        s_fin = per("s_fin", 3)
        s_h = per("s_h", 4)
        s_hturn = per("s_hturn", 4)
        s_hcopy = per("s_hcopy", 4)
        s_prod = per("s_prod", 4)
        s_node = per("s_node", 4)
        s_table = [[sem(f"s_table{i}{b}") for b in range(2)] for i in range(4)]

        SEEN0 = 22
        WEIGHED0 = 2 * NG
        SUMMED0 = 2
        NODEC = 2
        NODE0 = 2 * NODEC
        OWN = [16, 20]
        OWNS = sum(OWN)
        HALF = 2
        HC = [1, 2, 1, 1]
        HT0 = [2, 0, 0, 0]

        block = ctx.enter_context(nc.Block())

        def flat(ap):
            return ap.rearrange("h c -> (h c)")

        def bounds(eng, l, j):
            k = 4 if l == 1 else 0
            return (eng.value_load(plan[0:1, k, bass.ds(j, 1)], min_val=0, max_val=2 * PAIRS * MAXC),
                    eng.value_load(plan[0:1, k + 1, bass.ds(j, 1)], min_val=1, max_val=2 * PAIRS * MAXC))

        def pair_loop(eng, l, chunk_body, before, after):
            with eng.Fori(0, PAIRS) as j:
                first, end = bounds(eng, l, j)
                before(j)
                with eng.Fori(first, end) as g:
                    chunk_body(j, g, end)
                after(j, end)

        @block.sync
        def _(sp):
            sp.wait_ge(s_zeroed, 1)
            n = EFULL * EC
            for t, a in ((dst_all, dst), (src_all, src), (typ_all, etype), (wgt_all, eweight)):
                sp.dma_start(t[0:EFULL, :], a[0:n].rearrange("(p t) -> p t", t=EC)).then_inc(s_edges, 16)
                sp.dma_start(t[EFULL:EFULL + 1, 0:EREST], a[n:E].unsqueeze(0)).then_inc(s_edges, 16)
            sp.dma_start(nxt_all[0:EFULL, :], dst[1:n + 1].rearrange("(p t) -> p t", t=EC)).then_inc(s_edges, 16)
            sp.dma_start(nxt_all[EFULL:EFULL + 1, 0:EREST - 1], dst[n + 1:E].unsqueeze(0)).then_inc(s_edges, 16)
            sp.wait_ge(s_packed, 5)
            sp.dma_start(records[0:128 * EC, :].rearrange("(p t) c -> p t c", t=EC), rec_all[:, :, :]).then_inc(s_records, 16)
            sp.dma_start(records[128 * EC:EPAD, :].rearrange("(p t) c -> p t c", t=PADC), rec_pad[:, :, :]).then_inc(s_records, 16)
            sp.wait_ge(s_records, 32)
            sp.wait_ge(s_plan, 1)

            def load(l, b, g, start):
                if l < 2:
                    sp.wait_ge(s_seen, g * 20 + (10 * b + 3))
                else:
                    sp.wait_ge(s_summed[l], g * 2 + (b + 1))
                sp.dma_start(rec[b][:, :, :], records[bass.ds(start, CH), :].rearrange("(p t) c -> p t c", t=T)
                             ).then_inc(s_rec[l][b], 16)

            for l in range(4):
                if l >= 2:
                    sp.wait_ge(s_h[l], HC[l] * NT)
                with sp.Fori(0, PAIRS) as j:
                    first, end = bounds(sp, l, j)
                    run = [sp.value_load(plan[0:1, 2 + b, bass.ds(j, 1)], min_val=0, max_val=E) for b in range(2)]
                    with sp.Fori(first, end) as g:
                        for b in range(2):
                            load(l, b, g, nc.s_assert_within(
                                run[b] + (g - first) * CH, 0, EPAD - CH,
                                skip_runtime_bounds_check_because="a run starts at E at the latest and has at most MAXC chunks"))
                if l == 1:
                    load(1, 0, bounds(sp, 1, PAIRS - 1)[1], 0)
            sp.wait_ge(s_final, PAIRS)
            m = (NT - 1) * TN
            sp.dma_start(out[0:m, :].rearrange("(n p) d -> p n d", p=TN), X[:, 0:NT - 1, :]).then_inc(s_out, 16)
            sp.dma_start(out[m:N, :], X[0:LAST, NT - 1, :]).then_inc(s_out, 16)
            sp.wait_ge(s_out, 32)

        @block.gpsimd
        def _(pool):
            nc.gpsimd.memset(ident[:, :], 0.0).then_inc(s_iota, 1)
            nc.gpsimd.memset(pick[:, :, :], 0.0).then_inc(s_iota, 1)
            nc.gpsimd.iota(iota_i[:, :], pattern=[[1, TN]], base=0, channel_multiplier=0).then_inc(s_iota, 1)
            nc.gpsimd.iota(base_i[:, :], pattern=[[TN, NT + 1]], base=0, channel_multiplier=0).then_inc(s_iota, 1)
            nc.gpsimd.iota(steps_i[:, :], pattern=[[CH, MAXC - 1]], base=CH, channel_multiplier=0).then_inc(s_iota, 1)
            pool.wait_ge(s_iota, 5)
            nc.gpsimd.affine_select(out=ident[:, :], in_=ident[:, :], compare_op=ALU.not_equal, fill=1.0, base=0,
                                    pattern=[[-1, 128]], channel_multiplier=1).then_inc(s_const, 1)
            for k in range(PARTS):
                nc.gpsimd.affine_select(out=pick[:, :, :], in_=pick[:, :, :], compare_op=ALU.not_equal, fill=1.0, base=-k * T,
                                        pattern=[[-1, T], [0, TN]], channel_multiplier=1).then_inc(s_const, 1)
                pool.wait_ge(s_const, k + 2)
            pool.wait_ge(s_plan, 1)
            for l in range(4):
                table = gat_rows[l] if l < 2 else rel_rows[l - 2]
                c0 = 0 if l < 2 else 16
                pool.wait_ge(s_table[l][0], 16 * PAIRS + c0)
                pool.wait_ge(s_table[l][1], 16 * PAIRS + c0)
                with pool.Fori(0, PAIRS) as j:
                    first, end = bounds(pool, l, j)
                    with pool.Fori(first, end) as g:
                        for b in range(2):
                            if l < 2:
                                pool.wait_ge(s_weighed, g * (2 * NG) + (b + 1) * NG)
                            else:
                                pool.wait_ge(s_summed[l], g * 2 + (b + 1))
                            pool.sem_inc(s_pool, 1)
                            pool.wait_ge(s_rec[l][b], g * 16 + 16)
                            pool.sem_inc(s_pool, 1)
                            for t in range(T):
                                col = 0 if l < 2 else 1
                                rows = G[b][:, t, :] if l < 2 else G[b][:, t, 0:D]
                                nc.gpsimd.indirect_dma_start(
                                    rows, None, table,
                                    bass.IndirectOffsetOnAxis(ap=rec[b][:, t, col:col + 1], axis=0)
                                ).then_inc(s_rows[l][b], 16)

        @block.scalar
        def _(act):
            for t, a in ((w1, W1), (w2, W2)):
                act.dma_start(t[:, 0:D], a).then_inc(s_W, 16)
            for i, a in enumerate((b1, b2, c1, c2)):
                act.dma_start(bias[:, i, :], a.partition_broadcast(128)).then_inc(s_small, 16)
            for t, a, d in ((score1, as1, ad1), (score2, as2, ad2)):
                act.dma_start(t[:, 0:2, :].rearrange("p h c -> p (h c)"), flat(a).partition_broadcast(128)).then_inc(s_small, 16)
                act.dma_start(t[:, 2:4, :].rearrange("p h c -> p (h c)"), flat(d).partition_broadcast(128)).then_inc(s_small, 16)
            for i, a in enumerate((comp1, comp2)):
                act.dma_start(comp[:, i, :], flat(a).partition_broadcast(128)).then_inc(s_small, 16)
            m = (NT - 1) * TN
            act.wait_ge(s_zeroed, 2)
            act.dma_start(X[:, 0:NT - 1, :], x[0:m, :].rearrange("(n p) d -> p n d", p=TN)).then_inc(s_X, 16)
            act.dma_start(X[0:LAST, NT - 1, :], x[m:N, :]).then_inc(s_X, 16)
            act.dma_start(V[:, :, :], V1.rearrange("b i o -> i b o")).then_inc(s_V[0], 16)

            def node_pass(i, j):
                rel = i >= 2
                act.wait_ge(s_hturn[i], j * 2 + (2 + HT0[i]))
                for b in range(2):
                    nc.scalar.activation(hT[b][:, :], psF[0][:, b * 128:b * 128 + TN], ACT.Relu).then_inc(s_hcopy[i], 1)
                for b in range(2):
                    act.wait_ge(s_prod[i], j * 2 + (b + 1))
                    if rel:
                        act.wait_ge(s_table[i][b], j * 16 + 16)
                        for k in range(2):
                            nc.scalar.copy(tstage[b][:, k * 512:(k + 1) * 512], psF[k][0:TN, :]).then_inc(s_node[i], 1)
                        act.wait_ge(s_node[i], j * (2 * NODEC) + (NODE0 + NODEC * (b + 1)))
                        act.dma_start(rel_rows[i - 2][bass.ds((j * 2 + b) * (TN * R), TN * R), :].rearrange("(p r) d -> p (r d)", r=R),
                                      tstage[b][:, :]).then_inc(s_table[i][b], 16)
                    else:
                        row_ = Hn[i][:, bass.ds(j * 2 + b, 1), :].rearrange("p n w -> p (n w)")
                        nc.scalar.copy(row_[:, 0:2 * (C + 1)].rearrange("p (h c) -> p h c", h=2)[:, :, 0:C],
                                       psF[b][0:TN, 0:D].rearrange("p (h c) -> p h c", h=2)).then_inc(s_node[i], 1)
                        nc.scalar.copy(row_[:, 2 * (C + 1):HW], psF[b][0:TN, D:D + 4]).then_inc(s_node[i], 1)
                        act.wait_ge(s_node[i], j * (2 * NODEC) + (NODE0 + NODEC * (b + 1)))
                        act.dma_start(gat_rows[i][bass.ds((j * 2 + b) * TN, TN), :], row_[:, 0:GW]).then_inc(s_table[i][b], 16)

            for i in range(4):
                act.sem_inc(s_node[i], NODE0)
                if i >= 2:
                    for b in range(2):
                        act.sem_inc(s_table[i][b], 16)
            act.sem_inc(s_masks, 2)
            with act.Fori(0, PAIRS) as j:
                node_pass(0, j)
            act.wait_ge(s_plan, 1)

            def masks(slot, k, t0, t1):
                src_ = psT[(slot * NG + k) % 2][0:TN, 0:(t1 - t0) * 128].rearrange("p (t e) -> p t e", e=128)
                nc.scalar.copy(ST[slot][:, t0:t1, :], src_)
                nc.scalar.activation(SM[slot][:, t0:t1, :], src_, ACT.Copy, bias=-FAR, scale=FAR).then_inc(s_masks, 1)

            def next_masks(g, b, first, end):
                for k, t0, t1 in groups()[first:end]:
                    act.wait_ge(s_turned, g * (2 * NG) + ((b + 1) * NG + k + 1))
                    masks(1 - b, k, t0, t1)

            for k, t0, t1 in groups():
                act.wait_ge(s_turned, k + 1)
                masks(0, k, t0, t1)
            for l in range(2):
                if l == 1:
                    act.wait_ge(s_relw[0], 1)
                    act.dma_start(V[:, :, :], V2.rearrange("b i o -> i b o")).then_inc(s_V[1], 16)

                def chunk(j, g, end):
                    for b in range(2):
                        act.wait_ge(s_vturn, g * 2 + (b + 1))
                        nc.scalar.copy(vT[:, :, :].rearrange("p h e -> p (h e)"), vturned).then_inc(s_vrow, 1)
                        act.wait_ge(s_edgeval, g * 2 + (b + 1))
                        act.wait_ge(s_seen, g * 20 + (SEEN0 + 10 * b))
                        next_masks(g, b, 0, HALF)
                        act.wait_ge(s_expin, g * 4 + (2 * b + 1))
                        nc.scalar.activation(scl[:, b, :], dm[:, b, :], ACT.Exp).then_inc(s_expout, 1)
                        act.wait_ge(s_expin, g * 4 + (2 * b + 2))
                        nc.scalar.activation(p[:, :, :], z[:, 3, :, :], ACT.Exp).then_inc(s_expout, 1)
                        next_masks(g, b, HALF, NG)

                pair_loop(act, l, chunk, lambda j: None, lambda j, end: node_pass(l + 1, j))
            with act.Fori(0, PAIRS) as j:
                node_pass(3, j)

        @block.tensor
        def _(pe):
            def node_pass(i, j):
                pe.wait_ge(s_node[i], j * (2 * NODEC) + NODE0)
                for b in range(2):
                    pe.wait_ge(s_h[i], j * (2 * HC[i]) + HC[i] * (b + 1))
                    nc.tensor.transpose(psF[0][:, b * 128:b * 128 + TN], hb[b][:, :], ident[0:TN, 0:TN]).then_inc(s_hturn[i], 1)
                for b in range(2):
                    pe.wait_ge(s_hcopy[i], j * 2 + 2)
                    if i >= 2:
                        if b == 1:
                            pe.wait_ge(s_node[i], j * (2 * NODEC) + (NODE0 + NODEC))
                        for k in range(2):
                            mm = nc.tensor.matmul(psF[k][0:TN, :], hT[b][:, :],
                                                  rel_w[i - 2][:, 4 * k:4 * k + 4, :].rearrange("p r d -> p (r d)"),
                                                  start=True, stop=True)
                        mm.then_inc(s_prod[i], 1)
                    else:
                        nc.tensor.matmul(psF[b][0:TN, 0:D + 4], hT[b][:, :], (w1, w2)[i][:, :],
                                         start=True, stop=True).then_inc(s_prod[i], 1)

            pe.sem_inc(s_hturn[0], HT0[0])
            pe.sem_inc(s_edgeval, 1)
            for l in (1, 2, 3):
                pe.sem_inc(s_summed[l], SUMMED0)
            pe.wait_ge(s_counted, 1)
            nc.tensor.matmul(psA[0:1, 0:NT + 2], ones[:, 0:1], counts[:, :], start=True, stop=True).then_inc(s_counts, 1)
            pe.wait_ge(s_const, 1 + PARTS)
            pe.wait_ge(s_wext, 1)
            with pe.Fori(0, PAIRS) as j:
                node_pass(0, j)
            pe.wait_ge(s_plan, 1)

            def turn(slot, k, t0, t1):
                for t in range(t0, t1):
                    mm = nc.tensor.transpose(psT[(slot * NG + k) % 2][0:TN, (t - t0) * 128:(t - t0 + 1) * 128],
                                             S[slot][:, t, :], ident[:, :])
                mm.then_inc(s_turned, 1)

            pe.wait_ge(s_ident16, 1)
            def next_turn(l, g, b, k):
                pe.wait_ge(s_onehot[l], g * 4 + (2 * b + (3 if k < HALF else 4)))
                pe.wait_ge(s_masks, g * (2 * NG) + ((b + 1) * NG + k + 1))
                turn(1 - b, *groups()[k])

            pe.wait_ge(s_onehot[0], 2)
            for k, t0, t1 in groups():
                pe.wait_ge(s_masks, k + 1)
                turn(0, k, t0, t1)
            for l in range(2):
                if l == 1:
                    pe.wait_ge(s_relw[0], 1)

                def chunk(j, g, end):
                    for b in range(2):
                        pe.wait_ge(s_node[l + 1], j * (2 * NODEC) + NODE0)
                        pe.wait_ge(s_vparts, g * 2 + (b + 1))
                        pe.sem_inc(s_tensor, 1)
                        for h in range(H):
                            mm = nc.tensor.transpose(vturned[:, h * 128:(h + 1) * 128],
                                                     vp[:, h, :, :].rearrange("p k t -> p (k t)"), ident16[:, :])
                        mm.then_inc(s_vturn, 1)
                        pe.wait_ge(s_vrow, g * 2 + (b + 1))
                        for i, h, t0, t1 in spreads():
                            pe.wait_ge(s_seen, g * 20 + (10 * b + max(0, i - 2) + SEEN0))
                            for t in range(t0, t1):
                                mm = nc.tensor.matmul(psV[i % 3][0:TN, (t - t0) * 128:(t - t0 + 1) * 128],
                                                      pick[:, t, :], vT[:, h, :], start=True, stop=True)
                            mm.then_inc(s_spread, 1)
                            if i in (3, 5):
                                next_turn(l, g, b, (i - 3) // 2)
                        pe.wait_ge(s_masks, g * (2 * NG) + ((b + 1) * NG + 2))
                        pe.wait_ge(s_nodeval, g * 2 + (b + 1))
                        for t in range(T):
                            mm = nc.tensor.matmul(psE[:, 12 * t:12 * t + 12], ST[b][:, t, :],
                                                  nvp[:, :, :].rearrange("p k v -> p (k v)"), start=True, stop=True)
                        mm.then_inc(s_edgeval, 1)
                        for k in range(HALF, NG - 1):
                            next_turn(l, g, b, k)
                        for k, t0, t1 in groups():
                            if k == HALF:
                                next_turn(l, g, b, NG - 1)
                            pe.wait_ge(s_weighed, g * (2 * NG) + (b * NG + k + 1 + WEIGHED0))
                            for t in range(t0, t1):
                                mm = nc.tensor.matmul(psA[0:TN, 0:H * (C + 1)], S[b][:, t, :], Gs[:, t, :],
                                                      start=(t == 0), stop=(t == T - 1))
                        mm.then_inc(s_summed[l], 1)

                pair_loop(pe, l, chunk, lambda j: None, lambda j, end: node_pass(l + 1, j))

            pe.wait_ge(s_relw[1], 1)
            for l in range(2, 4):
                def chunk(j, g, end):
                    for b in range(2):
                        pe.wait_ge(s_onehot[l], g * 2 + (b + 1))
                        pe.wait_ge(s_rows[l][b], g * (16 * T) + 16 * T)
                        for t in range(T):
                            mm = nc.tensor.matmul((psA, psV[0])[b][0:TN, 0:D], S[b][:, t, :], G[b][:, t, 0:D],
                                                  start=(t == 0), stop=(t == T - 1))
                        mm.then_inc(s_summed[l], 1)

                pair_loop(pe, l, chunk, lambda j: None, lambda j, end: node_pass(l + 1, j) if l == 2 else None)

        @block.vector
        def _(dve):
            steps_done = [0]

            def link(ins):
                steps_done[0] += 1
                ins.then_inc(s_setup, 1)
                dve.wait_ge(s_setup, steps_done[0])

            nc.vector.memset(dst_all[:, :], 65536)
            nc.vector.memset(nxt_all[:, :], 65536)
            nc.vector.memset(src_all[:, :], 0)
            nc.vector.memset(typ_all[:, :], 0)
            nc.vector.memset(wgt_all[:, :], 0.0).then_inc(s_zeroed, 1)
            nc.vector.memset(X[:, NT - 1, :], 0.0).then_inc(s_zeroed, 1)
            nc.vector.memset(ones[:, :], 1.0)
            nc.vector.memset(counts[:, 0:1], 0.0)
            nc.vector.memset(rec_pad[:, :, :], 0)
            nc.vector.memset(Hn[0][:, :, :], 1.0)
            link(nc.vector.memset(Hn[1][:, :, :], 1.0))
            dve.wait_ge(s_iota, 5)
            nc.vector.tensor_copy(iota[:, :], iota_i[:, :])
            link(nc.vector.tensor_copy(base[:, :], base_i[:, :]))
            nc.vector.memset(base[:, NT:NT + 1], 0.0)
            nc.vector.tensor_copy(steps[:, :], steps_i[:, :])
            dve.sem_inc(s_seen, SEEN0)
            dve.sem_inc(s_weighed, WEIGHED0)

            def inverse_root(w, n):
                var, y, nhalf, t = (rstd[:, i, 0:n] for i in range(4))
                yield nc.vector.tensor_scalar(t.bitcast(I32), var.bitcast(I32), 1, None, ALU.logical_shift_right)
                yield nc.vector.tensor_scalar(y.bitcast(I32), t.bitcast(I32), -1.0, float(0x5f3759df), ALU.mult, ALU.add)
                yield nc.vector.tensor_scalar(nhalf, var, -0.5, None, ALU.mult)
                for _ in range(3):
                    yield nc.vector.tensor_tensor(t, y, y, ALU.mult)
                    yield nc.vector.tensor_tensor(t, t, nhalf, ALU.mult)
                    yield nc.vector.scalar_tensor_tensor(out=y, in0=t, scalar=1.5, in1=y, op0=ALU.add, op1=ALU.mult)

            dve.wait_ge(s_W, 32)
            dve.wait_ge(s_small, 16 * 10)
            for w, sc in ((w1, score1), (w2, score2)):
                for i in range(2):
                    link(nc.vector.tensor_tensor(prod[:, :], w[:, 0:D], sc[:, 2 * i:2 * i + 2, :].rearrange("p h c -> p (h c)"), ALU.mult))
                    ins = nc.vector.tensor_reduce(w[:, D + 2 * i:D + 2 * i + 2], prod[:, :].rearrange("p (h c) -> p h c", h=2), AX, ALU.add)
                    link(ins)
            dve.sem_inc(s_wext, 1)

            dve.wait_ge(s_X, 32)
            for n in range(NT):
                ins = nc.vector.bn_stats(stats[:, n, :], X[:, n, :])
            link(ins)
            for n in range(NT):
                ins = nc.vector.bn_aggr(mv[:, n, :], stats[:, n, :])
            link(ins)
            link(nc.vector.tensor_scalar(rstd[:, 0, :], mv[:, :, 1], EPS_LN, None, ALU.add))
            for ins in inverse_root(rstd, NT):
                link(ins)

            dve.wait_ge(s_edges, 16 * 10)
            nc.vector.tensor_copy(dst_f[:, :], dst_all[:, :])
            link(nc.vector.tensor_copy(nxt_f[:, :], nxt_all[:, :]))
            nc.vector.tensor_copy(rec_all[:, :, 0], src_all[:, :]).then_inc(s_packed, 1)
            nc.vector.scalar_tensor_tensor(out=rec_all[:, :, 1], in0=src_all[:, :], scalar=float(R), in1=typ_all[:, :],
                                           op0=ALU.mult, op1=ALU.add).then_inc(s_packed, 1)
            nc.vector.tensor_copy(rec_all[:, :, 2].bitcast(F32), dst_f[:, :]).then_inc(s_packed, 1)
            nc.vector.tensor_copy(rec_all[:, :, 3].bitcast(F32), wgt_all[:, :]).then_inc(s_packed, 1)
            nc.vector.memset(rec_pad[:, :, 2].bitcast(F32), 65536.0).then_inc(s_packed, 1)
            for k in range(1, NT + 1):
                link(nc.vector.tensor_scalar(scratch[:, :], dst_f[:, :], float(k * TN), None, ALU.is_lt, ALU.add,
                                             accum_out=counts[:, k:k + 1]))
            link(nc.vector.tensor_tensor(scratch[:, :], nxt_f[:, :], dst_f[:, :], ALU.is_lt))
            nc.vector.tensor_reduce(counts[:, NT + 1:NT + 2], scratch[:, :], AX, ALU.add).then_inc(s_counted, 1)

            dve.wait_ge(s_counts, 1)
            cnt, flag, lo, hi, size, nch, endr = (row[:, i, :] for i in range(7))
            link(nc.vector.tensor_copy(cnt, psA[0:1, 0:NT + 2]))
            link(nc.vector.tensor_scalar(flag[:, 0:1], cnt[:, NT + 1:NT + 2], 1.0, None, ALU.min))
            nc.vector.tensor_scalar(flag[:, 1:2], flag[:, 0:1], -1.0, 1.0, ALU.mult, ALU.add)
            link(nc.vector.tensor_scalar(flag[:, 2:3], flag[:, 0:1], float(E), None, ALU.mult))
            link(nc.vector.tensor_scalar(lo[:, 0:NT], cnt[:, 0:NT], flag[:, 1:2], None, ALU.mult))
            link(nc.vector.tensor_scalar(hi[:, 0:NT], cnt[:, 1:NT + 1], flag[:, 1:2], flag[:, 2:3], ALU.mult, ALU.add))
            link(nc.vector.tensor_tensor(size[:, 0:NT], hi[:, 0:NT], lo[:, 0:NT], ALU.subtract))
            pairs = size[:, 0:NT].rearrange("o (j b) -> o j b", b=2)
            link(nc.vector.tensor_tensor(hi[:, 0:PAIRS], pairs[:, :, 0], pairs[:, :, 1], ALU.max))
            link(nc.vector.tensor_tensor(over[:, :, :], hi[:, 0:PAIRS].unsqueeze(2).to_broadcast([1, PAIRS, MAXC - 1]),
                                         steps[:, :].unsqueeze(1).to_broadcast([1, PAIRS, MAXC - 1]), ALU.is_gt))
            link(nc.vector.tensor_reduce(nch[:, 0:PAIRS], over[:, :, :], AX, ALU.add))
            link(nc.vector.tensor_scalar(nch[:, 0:PAIRS], nch[:, 0:PAIRS], 1.0, None, ALU.add))
            link(nc.vector.tensor_tensor_scan(endr[:, 0:PAIRS], ones[0:1, 0:PAIRS], nch[:, 0:PAIRS], 0.0, ALU.mult, ALU.add))
            link(nc.vector.tensor_tensor(size[:, 0:PAIRS], endr[:, 0:PAIRS], nch[:, 0:PAIRS], ALU.subtract))
            runs = lo[:, 0:NT].rearrange("o (j b) -> o j b", b=2)
            nc.vector.tensor_copy(plan[:, 0, :], size[:, 0:PAIRS])
            nc.vector.tensor_copy(plan[:, 1, :], endr[:, 0:PAIRS])
            nc.vector.tensor_copy(plan[:, 2, :], runs[:, :, 0])
            nc.vector.tensor_copy(plan[:, 3, :], runs[:, :, 1])
            for i, part in ((4, size), (5, endr)):
                ins = nc.vector.tensor_scalar(plan[:, i, :], part[:, 0:PAIRS], endr[:, PAIRS - 1:PAIRS], None, ALU.add)
            ins.then_inc(s_plan, 1)

            with dve.Fori(0, PAIRS) as j:
                for b in range(2):
                    n = j * 2 + b
                    dve.wait_ge(s_hturn[0], n + 1)
                    nc.vector.tensor_scalar(hb[b][:, :], X[:, bass.ds(n, 1), :].rearrange("p n d -> p (n d)"),
                                            mv[:, bass.ds(n, 1), 0], rstd[:, 1, bass.ds(n, 1)],
                                            ALU.subtract, ALU.mult).then_inc(s_h[0], 1)
            dve.wait_ge(s_const, 1)
            nc.vector.tensor_copy(ident16[:, :], ident[:, :]).then_inc(s_ident16, 1)

            def relation_weights(i):
                dve.wait_ge(s_V[i], 16)
                for b in range(R):
                    for r in range(R):
                        c = comp[:, i, r * R + b:r * R + b + 1]
                        if b == 0:
                            ins = nc.vector.tensor_scalar(rel_w[i][:, r, :], V[:, b, :], c, None, ALU.mult)
                        else:
                            ins = nc.vector.scalar_tensor_tensor(out=rel_w[i][:, r, :], in0=V[:, b, :], scalar=c,
                                                                 in1=rel_w[i][:, r, :], op0=ALU.mult, op1=ALU.add)
                    if b < R - 1:
                        link(ins)
                ins.then_inc(s_relw[i], 1)

            def recs(b, c):
                return rec[b][:, :, c].bitcast(F32)

            seen, own = s_seen, s_own[0]

            def local(slot, tile):
                return nc.vector.tensor_scalar(dloc[:, slot, :], recs(slot, 2), base[:, bass.ds(tile, 1)], None, ALU.subtract)

            def onehots(slot, t0, t1):
                return nc.vector.tensor_tensor(S[slot][:, t0:t1, :], iota[:, :].unsqueeze(1).to_broadcast([128, t1 - t0, TN]),
                                               dloc[:, slot, t0:t1].unsqueeze(2).to_broadcast([128, t1 - t0, TN]), ALU.is_equal)

            dve.wait_ge(s_rec[0][0], 16)
            link(local(0, 0))
            onehots(0, 0, T).then_inc(s_onehot[0], 2)
            for l in range(2):
                relation_weights(l)
                dve.wait_ge(s_node[l], NODEC * NT + NODE0)

                def before(j):
                    node = Hn[l][:, bass.ds(j * 2, 2), :]
                    nc.vector.tensor_copy(M[:, :, :], node[:, :, 130:132]).then_inc(s_init[l], 1)
                    nc.vector.tensor_copy(nv[:, :, 0:2], node[:, :, 132:134]).then_inc(s_init[l], 1)
                    nc.vector.tensor_copy(acc[:, :, :], node[:, :, 0:130]).then_inc(s_init[l], 1)
                    nc.vector.tensor_tensor(zn[:, :, :], node[:, :, 130:132], node[:, :, 132:134], ALU.add).then_inc(s_init[l], 1)
                    dve.wait_ge(s_init[l], j * 5 + 4)
                    nc.vector.scalar_tensor_tensor(out=nv[:, :, 2:4], in0=zn[:, :, :], scalar=SLOPE, in1=zn[:, :, :],
                                                   op0=ALU.mult, op1=ALU.max).then_inc(s_init[l], 1)
                    dve.wait_ge(s_init[l], j * 5 + 5)
                    dve.sem_inc(s_vector, 1)

                def chunk(j, g, end):
                    for b in range(2):
                        steps_in = [b * OWN[0]]

                        def step(ins, wait=True):
                            steps_in[0] += 1
                            ins.then_inc(own, 1)
                            if wait:
                                dve.wait_ge(own, g * OWNS + steps_in[0])

                        def update(a):
                            dve.wait_ge(s_summed[l], g * 2 + (a + 1 + SUMMED0))
                            for h in range(H):
                                c0, c1_ = h * (C + 1), (h + 1) * (C + 1)
                                step(nc.vector.scalar_tensor_tensor(
                                    out=acc[:, a, c0:c1_], in0=acc[:, a, c0:c1_], scalar=scl[:, a, h:h + 1],
                                    in1=psA[0:TN, c0:c1_], op0=ALU.mult, op1=ALU.add), False)

                        dve.wait_ge(s_rows[l][b], g * (16 * T) + 16 * T)
                        scores = G[b][:, :, 130:132].rearrange("p t h -> p h t")
                        step(nc.vector.tensor_copy(vp[:, :, 0, :], scores))
                        step(nc.vector.tensor_tensor(vr[:, :, :], scores, vp[:, :, 0, :], ALU.subtract))
                        step(nc.vector.tensor_copy(vp[:, :, 1, :], vr[:, :, :]))
                        nc.vector.tensor_tensor(vp[:, :, 2, :], vr[:, :, :], vp[:, :, 1, :], ALU.subtract).then_inc(s_vparts, 1)
                        nxt = (j * 2 + 1) if b == 0 else nc.s_assert_within(
                            (j + (g + 1) // end) * 2, 0, NT, skip_runtime_bounds_check_because="g + 1 is end at most")
                        dve.wait_ge(s_rec[l][1 - b], g * 16 + 16 * (b + 1))
                        step(local(1 - b, nxt))
                        if b == 1:
                            update(0)
                        onehots(1 - b, 0, HALF * GRP).then_inc(s_onehot[l], 1)
                        dve.wait_ge(s_masks, g * (2 * NG) + (b * NG + NG + 2))
                        dve.sem_inc(s_vector, 1)
                        for i, h, t0, t1 in spreads():
                            dve.wait_ge(s_spread, g * 20 + (10 * b + i + 1))
                            dve.sem_inc(s_vector, 1)
                            w = (t1 - t0) * 128
                            nc.vector.tensor_tensor_reduce(
                                out=junk[:, i % 3, 0:w], in0=psV[i % 3][0:TN, 0:w], in1=SM[b][:, t0:t1, :].rearrange("p t e -> p (t e)"),
                                scale=1.0, scalar=-FAR, op0=ALU.add, op1=ALU.max, accum_out=mx[:, h, i // 2:i // 2 + 1]).then_inc(seen, 1)
                        dve.wait_ge(seen, g * 20 + (10 * b + 10 + SEEN0))
                        step(nc.vector.tensor_copy(mold[:, b, :], nv[:, b, 2:4]), False)
                        step(nc.vector.tensor_reduce(mc[:, :], mx[:, :, :], AX, ALU.max))
                        step(nc.vector.tensor_tensor(M[:, b, :], M[:, b, :], mc[:, :], ALU.max))
                        step(nc.vector.tensor_tensor(zn[:, b, :], M[:, b, :], nv[:, b, 0:2], ALU.add))
                        step(nc.vector.scalar_tensor_tensor(out=nv[:, b, 2:4], in0=zn[:, b, :], scalar=SLOPE, in1=zn[:, b, :],
                                                            op0=ALU.mult, op1=ALU.max))
                        step(nc.vector.tensor_copy(nvp[:, 0, :], nv[:, b, :]), False)
                        nc.vector.tensor_tensor(dm[:, b, :], mold[:, b, :], nv[:, b, 2:4], ALU.subtract).then_inc(s_expin, 1)
                        dve.wait_ge(own, g * OWNS + steps_in[0])
                        step(nc.vector.tensor_tensor(nvr[:, :], nv[:, b, :], nvp[:, 0, :], ALU.subtract))
                        step(nc.vector.tensor_copy(nvp[:, 1, :], nvr[:, :]))
                        nc.vector.tensor_tensor(nvp[:, 2, :], nvr[:, :], nvp[:, 1, :], ALU.subtract).then_inc(s_nodeval, 1)
                        onehots(1 - b, HALF * GRP, T).then_inc(s_onehot[l], 1)
                        at = psE.rearrange("p (t k v) -> p t v k", k=PARTS, v=4)
                        dve.wait_ge(s_edgeval, g * 2 + (b + 2))
                        step(nc.vector.tensor_reduce(ev[:, :, :], at, AX, ALU.add))
                        step(nc.vector.tensor_tensor(z[:, 0, :, :], ev[:, :, 0:2], G[b][:, :, 130:132], ALU.add))
                        step(nc.vector.scalar_tensor_tensor(out=z[:, 1, :, :], in0=z[:, 0, :, :], scalar=SLOPE, in1=z[:, 0, :, :],
                                                            op0=ALU.mult, op1=ALU.max))
                        step(nc.vector.tensor_tensor(z[:, 2, :, :], z[:, 1, :, :], ev[:, :, 2:4], ALU.subtract))
                        nc.vector.tensor_scalar(z[:, 3, :, :], z[:, 2, :, :], 0.0, None, ALU.min).then_inc(s_expin, 1)
                        dve.wait_ge(s_expout, g * 4 + (2 * b + 2))
                        for k, t0, t1 in groups():
                            nc.vector.tensor_tensor(
                                Gs[:, t0:t1, :].rearrange("p t (h c) -> p t h c", h=H),
                                G[b][:, t0:t1, 0:130].rearrange("p t (h c) -> p t h c", h=H),
                                p[:, t0:t1, :].unsqueeze(3).to_broadcast([128, t1 - t0, H, C + 1]),
                                ALU.mult).then_inc(s_weighed, 1)
                        if b == 1:
                            update(1)
                        assert steps_in[0] == sum(OWN[0:b + 1]), steps_in

                def after(j, end):
                    F = 2 if l == 0 else 19
                    done = [0]

                    def fin(ins, apart=False):
                        done[0] += 1
                        ins.then_inc(s_fin[l], 1)
                        dve.wait_ge(s_fin[l], j * F + done[0])
                        if apart:
                            dve.sem_inc(s_vector, 1)
                    dve.wait_ge(own, end * OWNS)
                    sums = acc[:, :, :].rearrange("p b (h c) -> p (b h) c", c=C + 1)
                    den = rs[:, 0, :, :].rearrange("p b h -> p (b h)")
                    inv = rs[:, 1, :, :].rearrange("p b h -> p (b h)")
                    fin(nc.vector.tensor_scalar(den.unsqueeze(2), sums[:, :, C:C + 1], 1e-16, None, ALU.add))
                    fin(nc.vector.reciprocal(inv, den))
                    for b in range(2):
                        for h in range(H):
                            target = hb[b] if l == 0 else o[:, b, :]
                            ins = nc.vector.scalar_tensor_tensor(
                                out=target[:, h * C:(h + 1) * C], in0=acc[:, b, h * (C + 1):h * (C + 1) + C],
                                scalar=rs[:, 1, b, h:h + 1], in1=bias[0:TN, l, h * C:(h + 1) * C], op0=ALU.mult, op1=ALU.add)
                            if l == 0:
                                ins.then_inc(s_h[1], 1)
                    if l == 0:
                        dve.wait_ge(s_h[1], j * (2 * HC[1]) + 2 * HC[1])
                        dve.sem_inc(s_vector, 1)
                        return
                    fin(ins)
                    for b in range(2):
                        xn = X[:, bass.ds(j * 2 + b, 1), :].rearrange("p n d -> p (n d)")
                        ins = nc.vector.scalar_tensor_tensor(out=xn, in0=o[:, b, :], scalar=0.0, in1=xn, op0=ALU.max, op1=ALU.add)
                    fin(ins, True)
                    for b in range(2):
                        ins = nc.vector.bn_stats(stats[:, b, :], X[:, bass.ds(j * 2 + b, 1), :].rearrange("p n d -> p (n d)"))
                    fin(ins, True)
                    for b in range(2):
                        ins = nc.vector.bn_aggr(mv[:, b, :], stats[:, b, :])
                    fin(ins)
                    fin(nc.vector.tensor_scalar(rstd[:, 0, 0:2], mv[:, 0:2, 1], EPS_LN, None, ALU.add))
                    for ins in inverse_root(rstd, 2):
                        fin(ins)
                    assert done[0] == F, done
                    for b in range(2):
                        nc.vector.tensor_scalar(hb[b][:, :], X[:, bass.ds(j * 2 + b, 1), :].rearrange("p n d -> p (n d)"),
                                                mv[:, b, 0:1], rstd[:, 1, b:b + 1], ALU.subtract, ALU.mult).then_inc(s_h[2], 1)
                    dve.wait_ge(s_h[2], j * 2 + 2)
                    dve.sem_inc(s_vector, 1)

                pair_loop(dve, l, chunk, before, after)

            dve.wait_ge(s_masks, bounds(dve, 1, PAIRS - 1)[1] * (2 * NG) + (NG + 2))
            dve.sem_inc(s_vector, 1)
            for l in range(2, 4):
                def before(j):
                    for b in range(2):
                        if l == 2:
                            nc.vector.tensor_copy(acc[:, b, 0:D], bias[0:TN, l, :]).then_inc(s_init[l], 1)
                        else:
                            nc.vector.tensor_tensor(acc[:, b, 0:D], X[:, bass.ds(j * 2 + b, 1), :].rearrange("p n d -> p (n d)"),
                                                    bias[0:TN, l, :], ALU.add).then_inc(s_init[l], 1)
                    dve.wait_ge(s_init[l], j * 2 + 2)
                    dve.sem_inc(s_vector, 1)

                def chunk(j, g, end):
                    for b in range(2):
                        dve.wait_ge(s_rec[l][b], g * 16 + 16)
                        nc.vector.tensor_scalar(dloc[:, b, :], recs(b, 2), base[:, bass.ds(j * 2 + b, 1)], None,
                                                ALU.subtract).then_inc(s_own[l], 1)
                        dve.wait_ge(s_own[l], g * 4 + (2 * b + 1))
                        for t in range(T):
                            ins = nc.vector.tensor_scalar(S[b][:, t, :], iota[:, :], dloc[:, b, t:t + 1], recs(b, 3)[:, t:t + 1],
                                                          ALU.is_equal, ALU.mult)
                        ins.then_inc(s_onehot[l], 1)
                        dve.wait_ge(s_summed[l], g * 2 + (b + 1 + SUMMED0))
                        nc.vector.tensor_tensor(acc[:, b, 0:D], acc[:, b, 0:D], (psA, psV[0])[b][0:TN, 0:D], ALU.add).then_inc(s_own[l], 1)

                def after(j, end):
                    dve.wait_ge(s_own[l], end * 4)
                    dve.sem_inc(s_vector, 1)
                    for b in range(2):
                        if l == 2:
                            nc.vector.tensor_copy(hb[b][:, :], acc[:, b, 0:D]).then_inc(s_h[3], 1)
                        else:
                            ins = nc.vector.tensor_copy(X[:, bass.ds(j * 2 + b, 1), :].rearrange("p n d -> p (n d)"), acc[:, b, 0:D])
                    if l == 3:
                        ins.then_inc(s_final, 1)
                    dve.wait_ge(s_h[3] if l == 2 else s_final, j * 2 + 2 if l == 2 else j + 1)
                    dve.sem_inc(s_vector, 1)

                pair_loop(dve, l, chunk, before, after)


_INS = ["x", "src", "dst", "edge_type_8", "edge_weight", "L0_gnn_W1", "L0_gnn_a_src1", "L0_gnn_a_dst1", "L0_gnn_b1",
        "L0_gnn_W2", "L0_gnn_a_src2", "L0_gnn_a_dst2", "L0_gnn_b2", "L1_gnn_comp1", "L1_gnn_V1", "L1_gnn_bias1",
        "L1_gnn_comp2", "L1_gnn_V2", "L1_gnn_bias2"]


def kernel(**inputs):
    import numpy as _np
    import concourse.bacc as _bacc
    from concourse import mybir as _mybir
    from concourse.bass_utils import run_bass_kernel_spmd as _run

    nc = _bacc.Bacc("TRN2", target_bir_lowering=False, num_devices=1)
    arrays, args = {}, []
    for name in _INS:
        a = _np.ascontiguousarray(inputs[name])
        arrays[f"in_{name}_dram"] = a
        args.append(nc.dram_tensor(f"in_{name}_dram", a.shape, _mybir.dt.from_np(a.dtype), kind="ExternalInput").ap())
    out = nc.dram_tensor("out_0_dram", (N, D), _mybir.dt.float32, kind="ExternalOutput").ap()
    build(nc, *args, out)
    r = _run(nc, [arrays], core_ids=[0])
    return r.results[0]["out_0_dram"]
```
